# Optimizing a Trainium2 kernel written in Bass

```python
import numpy as np
import jax
import jax.numpy as jnp

def _softmax(x, axis=-1):
    return jax.nn.softmax(x, axis=axis)

def _gelu(x):
    return jax.nn.gelu(x, approximate=True)

def _silu(x):
    return jax.nn.silu(x)

def _sigmoid(x):
    return jax.nn.sigmoid(x)

def _layernorm(x, axis=-1, eps=1e-05):
    m = jnp.mean(x, axis=axis, keepdims=True)
    v = jnp.var(x, axis=axis, keepdims=True)
    return (x - m) / jnp.sqrt(v + eps)

def _scatter_add(tgt, idx, src, axis=0):
    return tgt.at[idx].add(src)

def _segment_sum(src, seg, n):
    return jax.ops.segment_sum(src, seg, n)
kernel_name = 'mk_adj_resnorm_d2_adj_r2_d81ae5'

def setup_inputs(seed: int=0):
    np.random.seed(seed)
    _w = jnp.asarray

    def _rec_inputs():
        import jax
        import jax.numpy as jnp
        _gk = jax.random.key(seed)
        x = -0.000125 + 0.9999 * jax.random.normal(jax.random.fold_in(_gk, 1), (128, 64, 512), jnp.float32)
        _w = (1.0 + jnp.arange(64, dtype=jnp.float32)) ** (-0.5)
        _w = _w / _w.mean()
        _pij = jnp.clip(0.125 * _w[:, None] * _w[None, :], 0.0, 1.0)
        _a = jax.random.uniform(jax.random.fold_in(_gk, 2), (64, 64)) < _pij
        adj = _a.astype(jnp.int32)
        return (x, adj)
    x, adj = _rec_inputs()

    def _L0_gnn_setup():
        import jax, jax.numpy as jnp
        import numpy as np
        B, N, E, H = (64, 256, 512, 16)
        DH = E // H
        key = jax.random.key(seed)
        ks = jax.random.split(key, 5)
        x = jax.random.normal(ks[0], (B, N, E), dtype=jnp.float32)
        Wqkv = jax.random.normal(ks[1], (E, 3 * E), dtype=jnp.float32) * 0.02
        bqkv = jnp.zeros((3 * E,), dtype=jnp.float32)
        Wproj = jax.random.normal(ks[2], (E, E), dtype=jnp.float32) * 0.02
        bproj = jnp.zeros((E,), dtype=jnp.float32)
        adj = jax.random.randint(ks[3], (N, N), 0, 2, dtype=jnp.int32)
        return {'x': x, 'Wqkv': Wqkv, 'bqkv': bqkv, 'Wproj': Wproj, 'bproj': bproj, 'adj': adj}
    _L0_gnn_all = _L0_gnn_setup()
    _L0_gnn_in = {k: v for k, v in _L0_gnn_all.items() if k in ('Wqkv', 'bqkv', 'Wproj', 'bproj')}
    del _L0_gnn_all

    def _L1_gnn_setup():
        import jax, jax.numpy as jnp
        import numpy as np
        B, N, E, H = (64, 256, 512, 16)
        DH = E // H
        key = jax.random.key(seed)
        ks = jax.random.split(key, 5)
        x = jax.random.normal(ks[0], (B, N, E), dtype=jnp.float32)
        Wqkv = jax.random.normal(ks[1], (E, 3 * E), dtype=jnp.float32) * 0.02
        bqkv = jnp.zeros((3 * E,), dtype=jnp.float32)
        Wproj = jax.random.normal(ks[2], (E, E), dtype=jnp.float32) * 0.02
        bproj = jnp.zeros((E,), dtype=jnp.float32)
        adj = jax.random.randint(ks[3], (N, N), 0, 2, dtype=jnp.int32)
        return {'x': x, 'Wqkv': Wqkv, 'bqkv': bqkv, 'Wproj': Wproj, 'bproj': bproj, 'adj': adj}
    _L1_gnn_all = _L1_gnn_setup()
    _L1_gnn_in = {k: v for k, v in _L1_gnn_all.items() if k in ('Wqkv', 'bqkv', 'Wproj', 'bproj')}
    del _L1_gnn_all
    return {'x': x, 'adj': adj, 'L0_gnn_Wqkv': _L0_gnn_in['Wqkv'], 'L0_gnn_bqkv': _L0_gnn_in['bqkv'], 'L0_gnn_Wproj': _L0_gnn_in['Wproj'], 'L0_gnn_bproj': _L0_gnn_in['bproj'], 'L1_gnn_Wqkv': _L1_gnn_in['Wqkv'], 'L1_gnn_bqkv': _L1_gnn_in['bqkv'], 'L1_gnn_Wproj': _L1_gnn_in['Wproj'], 'L1_gnn_bproj': _L1_gnn_in['bproj']}

def reference(x, adj, L0_gnn_Wqkv, L0_gnn_bqkv, L0_gnn_Wproj, L0_gnn_bproj, L1_gnn_Wqkv, L1_gnn_bqkv, L1_gnn_Wproj, L1_gnn_bproj):
    import jax
    import jax.numpy as jnp

    def _L0_gnn_ref(x, Wqkv, bqkv, Wproj, bproj, adj):
        import jax, jax.numpy as jnp
        import numpy as np
        B, N, E, H = (64, 256, 512, 16)
        DH = E // H
        b, n, e = x.shape
        h, dh = (H, e // H)
        qkv = (x @ Wqkv + bqkv).reshape(b, n, 3, h, dh)
        qkv = jnp.transpose(qkv, (2, 0, 3, 1, 4))
        q, k, v = (qkv[0], qkv[1], qkv[2])
        mask = adj + jnp.eye(n, dtype=adj.dtype) > 0
        scale = 1.0 / jnp.sqrt(jnp.asarray(dh, dtype=x.dtype))
        scores = jnp.einsum('bhnd,bhmd->bhnm', q, k) * scale
        scores = jnp.where(mask[None, None], scores, jnp.finfo(scores.dtype).min)
        attn = jax.nn.softmax(scores, axis=-1)
        y = jnp.einsum('bhnm,bhmd->bhnd', attn, v)
        y = jnp.transpose(y, (0, 2, 1, 3)).reshape(b, n, e)
        return y @ Wproj + bproj

    def _L1_gnn_ref(x, Wqkv, bqkv, Wproj, bproj, adj):
        import jax, jax.numpy as jnp
        import numpy as np
        B, N, E, H = (64, 256, 512, 16)
        DH = E // H
        b, n, e = x.shape
        h, dh = (H, e // H)
        qkv = (x @ Wqkv + bqkv).reshape(b, n, 3, h, dh)
        qkv = jnp.transpose(qkv, (2, 0, 3, 1, 4))
        q, k, v = (qkv[0], qkv[1], qkv[2])
        mask = adj + jnp.eye(n, dtype=adj.dtype) > 0
        scale = 1.0 / jnp.sqrt(jnp.asarray(dh, dtype=x.dtype))
        scores = jnp.einsum('bhnd,bhmd->bhnm', q, k) * scale
        scores = jnp.where(mask[None, None], scores, jnp.finfo(scores.dtype).min)
        attn = jax.nn.softmax(scores, axis=-1)
        y = jnp.einsum('bhnm,bhmd->bhnd', attn, v)
        y = jnp.transpose(y, (0, 2, 1, 3)).reshape(b, n, e)
        return y @ Wproj + bproj
    x = _layernorm(x + _L0_gnn_ref(x, L0_gnn_Wqkv, L0_gnn_bqkv, L0_gnn_Wproj, L0_gnn_bproj, adj), axis=-1)
    x = _layernorm(x + _L1_gnn_ref(x, L1_gnn_Wqkv, L1_gnn_bqkv, L1_gnn_Wproj, L1_gnn_bproj, adj), axis=-1)
    return x

_drawn_inputs = setup_inputs


def setup_inputs(seed=0):
    import zlib

    import numpy as np

    out = dict(_drawn_inputs(seed))
    spreads = {'L0_gnn_bqkv': (0.0, 0.1),
     'L0_gnn_bproj': (0.0, 0.1),
     'L1_gnn_bqkv': (0.0, 0.1),
     'L1_gnn_bproj': (0.0, 0.1)}
    factors = {}
    for name, (base, spread) in spreads.items():
        noise = np.random.default_rng([zlib.crc32(name.encode()), seed]).standard_normal(out[name].shape)
        drawn = base * np.exp(spread * noise) if base else spread * noise
        out[name] = jnp.asarray(drawn.astype(out[name].dtype))
    for name, factor in factors.items():
        out[name] = (out[name] * factor).astype(out[name].dtype)
    return out
```

```python
import numpy as np

import concourse.bass as bass
from concourse import mybir
from contextlib import ExitStack

FP32 = mybir.dt.float32
FP32R = mybir.dt.float32r
INT32 = mybir.dt.int32
ALU = mybir.AluOpType
ACT = mybir.ActivationFunctionType
AX = mybir.AxisListType

GRAPHS, NODES, E, H = 128, 64, 512, 16
DH = E // H
P = 128
LAYERS = 2
Q = 32
PAIRS = GRAPHS * NODES // P
GROUP = 4
TOK = GROUP * P
KT = E // P
HG = P // DH
HALVES = NODES // Q
SLOTS = LAYERS * PAIRS
AHEAD = 2 * GROUP
LOAD = AHEAD + 2
X_RING = 4
UNROLL = 2 * GROUP
LOOPS = PAIRS // UNROLL - 1
TILES = 2 * KT
QKA = [1, 3, 5, 7]
QKB = [2, 4, 6, TILES]
SCALE = float(DH) ** -0.5
EPS = 1e-5
MASKED = 3.0e38
LOADED = 16


def gnn_kernel(nc, x, adj, ident, eye, weights, out):
    ctx = ExitStack()
    with ctx:
        def sb(name, shape, dt=FP32):
            return ctx.enter_context(nc.sbuf_tensor(name, shape, dt))

        def pb(name, shape):
            return ctx.enter_context(nc.psum_tensor(name, shape, FP32))

        def sem(name):
            return ctx.enter_context(nc.semaphore(name))

        hidden = nc.dram_tensor("hidden", [PAIRS * P, E], FP32, kind="Internal").ap()
        sources = [x, hidden]
        targets = [hidden, out]

        w_stage = sb("w_stage", [P, KT, 2 * E])
        wqk_h = sb("wqk_h", [P, KT, 2 * E], FP32R)
        wqk_l = sb("wqk_l", [P, KT, 2 * E], FP32R)
        wv_h = sb("wv_h", [P, KT, E], FP32R)
        wv_l = sb("wv_l", [P, KT, E], FP32R)
        wp_h = sb("wp_h", [P, KT, E], FP32R)
        wp_l = sb("wp_l", [P, KT, E], FP32R)
        b_qk = sb("b_qk", [P, LAYERS, TILES])
        b_v = sb("b_v", [P, LAYERS, E])
        b_p = sb("b_p", [P, LAYERS, E])
        idn = sb("idn", [P, P])
        adj_i = sb("adj_i", [P, NODES], INT32)
        eye_s = sb("eye_s", [P, NODES])
        mask = sb("mask", [P, NODES])
        minus_half = sb("minus_half", [P, 1])

        x_in = [sb(f"x_in{b}", [P, E]) for b in range(4)]
        xt_h = [sb(f"xt_h{b}", [P, KT, TOK], FP32R) for b in range(2)]
        xt_l = [sb(f"xt_l{b}", [P, KT, TOK], FP32R) for b in range(2)]
        q_t = [sb(f"q_t{b}", [P, KT, TOK]) for b in range(2)]
        k_t = [sb(f"k_t{b}", [P, KT, TOK]) for b in range(2)]
        k_x = sb("k_x", [P, KT, HG, P])
        v_s = [sb(f"v_s{b}", [P, E]) for b in range(2)]
        t_s = sb("t_s", [P, H * NODES])
        e_s = sb("e_s", [P, H * NODES])
        p_t = sb("p_t", [P, H, 2, NODES])
        y_h = sb("y_h", [P, E], FP32R)
        y_l = sb("y_l", [P, E], FP32R)
        x_res = [sb(f"x_res{b}", [P, E]) for b in range(2)]
        z_out = [sb(f"z_out{b}", [P, E]) for b in range(2)]
        red = sb("red", [P, H * HALVES])
        red_x = sb("red_x", [P, H * HALVES])
        row_max = sb("row_max", [P, H * HALVES])
        row_sum = sb("row_sum", [P, H * HALVES])
        row_inv = sb("row_inv", [P, H * HALVES])
        stats = sb("stats", [P, 6])
        mean_var = [sb(f"mean_var{b}", [P, 2]) for b in range(2)]
        var_eps = sb("var_eps", [P, 1])
        rstd = [sb(f"rstd{b}", [P, 1]) for b in range(2)]
        shift = [sb(f"shift{b}", [P, 1]) for b in range(2)]

        ps_s = pb("ps_s", [P, H * NODES])
        ps_qk = [pb(f"ps_qk{b}", [P, TOK]) for b in range(2)]
        ps_v = pb("ps_v", [P, E])
        ps_t = pb("ps_t", [P, KT * P])
        ps_y = pb("ps_y", [P, E])
        ps_z = pb("ps_z", [P, E])

        const_in = sem("const_in")
        bias_in = sem("bias_in")
        w_in = sem("w_in")
        x_loaded = [sem(f"x_loaded{b}") for b in range(4)]
        res_loaded = [sem(f"res_loaded{b}") for b in range(2)]
        stored = [sem(f"stored{b}") for b in range(2)]
        zeroed = sem("zeroed")
        mask_step = sem("mask_step")
        w_high = sem("w_high")
        w_low = sem("w_low")
        qk_done = sem("qk_done")
        v_done = sem("v_done")
        t_done = sem("t_done")
        s_done = sem("s_done")
        pv_done = sem("pv_done")
        proj_done = sem("proj_done")
        qk_kept = sem("qk_kept")
        xh_kept = sem("xh_kept")
        xt_kept = sem("xt_kept")
        kx_built = sem("kx_built")
        v_kept = sem("v_kept")
        masked = sem("masked")
        dve_step = sem("dve_step")
        shifted = sem("shifted")
        exp_done = sem("exp_done")
        inv_ready = sem("inv_ready")
        normed = sem("normed")
        pt_ready = sem("pt_ready")
        yh_kept = sem("yh_kept")
        yl_kept = sem("yl_kept")
        xb_ready = sem("xb_ready")
        z_ready = sem("z_ready")
        var_ready = sem("var_ready")
        pool_step = sem("pool_step")
        rstd_ready = sem("rstd_ready")
        out_ready = sem("out_ready")

        V_CREDIT = YL_CREDIT = Z_CREDIT = 1
        DVE_STEPS = 14
        POOL_STEPS = 2
        W_STEPS = 3

        class Slot:

            def __init__(self, layer, j, k):
                self.layer, self.j, self.k = layer, j, k
                self.p = k % GROUP
                self.last = not isinstance(j, int) or layer * PAIRS + UNROLL * j + k
                self.fixed = isinstance(j, int)

            def count(self, plus=0, each=1):
                return self.j * (UNROLL * each) + each * (self.layer * PAIRS + self.k + plus)

            def ring(self, plus, size, more=0):
                c = (self.layer * PAIRS + self.k + plus) // size + 1 + more
                return self.j * (UNROLL // size * LOADED) + LOADED * c

            def tiles(self, t):
                g = (self.layer * PAIRS + self.k) // GROUP + 1
                return self.j * (UNROLL // GROUP * TILES) + TILES * g + t + 1

            def tile_pair(self, t):
                return GROUP * (1 + t // TILES) - self.p

            def has(self, plus):
                return not self.fixed or self.count(plus) < SLOTS

            def pair(self, plus):
                m = self.layer * PAIRS + self.k + plus
                if self.fixed:
                    m += UNROLL * self.j
                    return m // PAIRS, (m % PAIRS) * P
                return self.layer, self.j * (UNROLL * P) + (self.k + plus) * P

        def run_slots(eng, slot, between=None, loops=LOOPS):
            for layer in range(LAYERS):
                with eng.Fori(0, loops) as j:
                    for k in range(UNROLL):
                        slot(Slot(layer, j, k))
                for j in range(loops, PAIRS // UNROLL):
                    for k in range(UNROLL):
                        slot(Slot(layer, j, k))
                if between is not None and layer + 1 < LAYERS:
                    between(layer + 1)

        def graph_rows(tile, p, g):
            return tile[:, g, p * P:(p + 1) * P]

        block = ctx.enter_context(nc.Block())

        passed = sem("passed")
        CONSTS = 6 * LOADED

        @block.sync
        def _(sp):
            def load_x(layer, row, b, count):
                sp.dma_start(x_in[b][:], sources[layer][bass.ds(row, P), :]).then_inc(x_loaded[b], LOADED)

            def load_w_qk(layer):
                w = weights[layer][0].rearrange("(t p) n -> p t n", p=P)
                sp.dma_start(w_stage[:], w[:, :, 0:2 * E]).then_inc(w_in, LOADED)

            def load_w_rest(layer):
                w = weights[layer][0].rearrange("(t p) n -> p t n", p=P)
                wp = weights[layer][2].rearrange("(t p) n -> p t n", p=P)
                sp.dma_start(w_stage[:, :, 0:E], w[:, :, 2 * E:3 * E]).then_inc(w_in, LOADED)
                sp.dma_start(w_stage[:, :, E:2 * E], wp).then_inc(w_in, LOADED)

            sp.sem_inc(stored[0], LOADED)
            sp.sem_inc(stored[1], LOADED)
            sp.dma_start(idn[:], ident).then_inc(const_in, LOADED)
            for m in range(4):
                load_x(0, m * P, m, m)
            load_w_qk(0)
            sp.dma_start(eye_s[:], eye).then_inc(const_in, LOADED)
            for b in range(2):
                for mh in range(HALVES):
                    r = Q * (HALVES * b + mh)
                    src = adj.rearrange("(a n) m -> n a m", a=HALVES)[:, :, Q * mh:Q * mh + Q]
                    dst = adj_i[r:r + Q, :].rearrange("p (a m) -> p a m", a=HALVES)
                    sp.dma_start(dst, src).then_inc(const_in, LOADED)
            with nc.allow_non_contiguous_dma(reason="biases by partition, once"):
                for layer in range(LAYERS):
                    b = weights[layer][1]
                    sp.dma_start(b_qk[:, layer, 0:KT], b[E:2 * E].rearrange("(t p) -> p t", p=P)).then_inc(bias_in, LOADED)
                    sp.dma_start(b_qk[:, layer, KT:TILES], b[0:E].rearrange("(t p) -> p t", p=P)).then_inc(bias_in, LOADED)
                    sp.dma_start(b_v[:, layer, :], b[2 * E:3 * E].unsqueeze(0).to_broadcast([P, E])).then_inc(bias_in, LOADED)
                    sp.dma_start(b_p[:, layer, :], weights[layer][3].unsqueeze(0).to_broadcast([P, E])).then_inc(bias_in, LOADED)
            sp.dma_start(x_res[0][:], sources[0][0:P, :]).then_inc(res_loaded[0], LOADED)
            for m in range(4, LOAD):
                sp.wait_ge(t_done, m - 3)
                load_x(0, m * P, m % 4, m)
            sp.wait_ge(w_low, 1)
            load_w_rest(0)

            def slot(s):
                if s.fixed and s.j == LOOPS and s.layer + 1 < LAYERS and s.k == 0:
                    sp.wait_ge(w_low, W_STEPS * (s.layer + 1))
                    load_w_qk(s.layer + 1)
                if s.has(LOAD):
                    sp.wait_ge(t_done, s.count(LOAD - 3))
                    sp.sem_inc(passed, 1)
                    layer, row = s.pair(LOAD)
                    if layer > 0:
                        sp.wait_ge(stored[s.k % 2], s.ring(LOAD - PAIRS, 2, 1))
                        sp.sem_inc(passed, 1)
                    load_x(layer, row, (s.k + LOAD) % 4, None)
                if s.has(1):
                    sp.wait_ge(out_ready, s.count(0) + Z_CREDIT)
                    sp.sem_inc(passed, 1)
                    layer, row = s.pair(1)
                    if layer > 0:
                        sp.wait_ge(stored[(s.k + 1) % 2], s.ring(1 - PAIRS, 2, 1))
                        sp.sem_inc(passed, 1)
                    sp.dma_start(x_res[(s.k + 1) % 2][:], sources[layer][bass.ds(row, P), :]
                                 ).then_inc(res_loaded[(s.k + 1) % 2], LOADED)
                sp.wait_ge(out_ready, s.count(1) + Z_CREDIT)
                sp.sem_inc(passed, 1)
                layer, row = s.pair(0)
                sp.dma_start(targets[layer][bass.ds(row, P), :], z_out[s.k % 2][:]
                             ).then_inc(stored[s.k % 2], LOADED)
                if s.fixed and s.j == LOOPS and s.layer + 1 < LAYERS and s.k == GROUP:
                    sp.wait_ge(w_low, W_STEPS * (s.layer + 1) + 1)
                    load_w_rest(s.layer + 1)

            run_slots(sp, slot, loops=LOOPS - 1)
            for b in range(2):
                sp.wait_ge(stored[b], LOADED * (SLOTS // 2 + 1))

        @block.tensor
        def _(pe):
            def dense(ps, lhs_h, lhs_l, rhs_h, rhs_l):
                for t in range(KT):
                    nc.tensor.matmul(ps, lhs_l(t), rhs_h(t), start=(t == 0), stop=False)
                    nc.tensor.matmul(ps, lhs_h(t), rhs_l(t), start=False, stop=False)
                    last = nc.tensor.matmul(ps, lhs_h(t), rhs_h(t), start=False, stop=(t == KT - 1))
                return last

            def transpose_x(b):
                for t in range(KT):
                    last = nc.tensor.transpose(ps_t[:, t * P:(t + 1) * P], x_in[b][:, t * P:(t + 1) * P], idn[:])
                last.then_inc(t_done, 1)

            def qk_tile(t, par, count):
                par, t = (par + t // TILES) % 2, t % TILES
                c0 = E + t * P if t < KT else (t - KT) * P
                if isinstance(count, int) and count <= 2:
                    pass
                else:
                    pe.wait_ge(qk_kept, count - 2)
                dense(ps_qk[t % 2][:],
                      lambda r: wqk_h[:, r, c0:c0 + P], lambda r: wqk_l[:, r, c0:c0 + P],
                      lambda r: xt_h[par][:, r, :], lambda r: xt_l[par][:, r, :]).then_inc(qk_done, 1)

            def scores(par, p):
                for g in range(KT):
                    for nh in range(HALVES):
                        for qd in range(4):
                            b, mh = qd // 2, qd % 2
                            n0 = p * P + b * NODES + nh * Q
                            m0 = b * NODES + mh * Q
                            dst = ps_s[Q * qd:Q * qd + Q, :].rearrange("p (h c) -> p h c", h=H)
                            last = nc.tensor.matmul(
                                dst[:, HG * g:HG * g + HG, nh * Q:nh * Q + Q],
                                q_t[par][:, g, n0:n0 + Q], k_x[:, g, :, m0:m0 + Q],
                                start=True, stop=True)
                last.then_inc(s_done, 1)

            pe.wait_ge(const_in, CONSTS)
            for m in range(AHEAD):
                pe.wait_ge(x_loaded[m % 4], LOADED * (m // 4 + 1))
                if m:
                    pe.wait_ge(xt_kept, m)
                transpose_x(m % 4)
            pe.wait_ge(w_low, 1)
            for t in range(TILES):
                qk_tile(t, 0, t + 1)
            pe.wait_ge(qk_kept, TILES)
            pe.wait_ge(kx_built, 1)
            scores(0, 0)
            qk_tile(TILES, 0, TILES + 1)

            def slot(s):
                par = (s.k // GROUP) % 2
                if s.has(s.tile_pair(QKA[s.p])):
                    qk_tile(QKA[s.p], 1 - par, s.tiles(QKA[s.p]))

                if s.k == 0:
                    pe.wait_ge(w_low, W_STEPS * s.layer + 2)
                pe.wait_ge(v_kept, s.count(0) + V_CREDIT)
                tok = slice(s.p * P, s.p * P + P)
                dense(ps_v[:],
                      lambda r: xt_h[par][:, r, tok], lambda r: xt_l[par][:, r, tok],
                      lambda r: wv_h[:, r, :], lambda r: wv_l[:, r, :]).then_inc(v_done, 1)

                if s.has(AHEAD):
                    pe.wait_ge(x_loaded[s.k % 4], s.ring(AHEAD, 4))
                    pe.wait_ge(xt_kept, s.count(AHEAD))
                    transpose_x(s.k % 4)

                if s.has(1):
                    if s.p == GROUP - 1:
                        pe.wait_ge(qk_kept, s.tiles(TILES - 1))
                    pe.wait_ge(kx_built, s.count(2))
                    pe.wait_ge(masked, s.count(1))
                    scores(((s.k + 1) // GROUP) % 2, (s.k + 1) % GROUP)

                pe.wait_ge(v_kept, s.count(1) + V_CREDIT)
                pe.wait_ge(pt_ready, s.count(1))
                pe.wait_ge(yl_kept, s.count(0) + YL_CREDIT)
                for g in range(KT):
                    for hh in range(HG):
                        h = HG * g + hh
                        last = nc.tensor.matmul(ps_y[DH * hh:DH * hh + DH, g * P:(g + 1) * P],
                                                v_s[s.k % 2][:, DH * h:DH * h + DH],
                                                p_t[:, h, :, :].rearrange("p b n -> p (b n)"),
                                                start=True, stop=True)
                last.then_inc(pv_done, 1)

                if s.has(s.tile_pair(QKB[s.p])):
                    if s.p == GROUP - 1:
                        pe.wait_ge(xt_kept, s.count(AHEAD + 1))
                        if s.fixed and s.k == GROUP - 1 and s.layer + 1 < LAYERS:
                            pe.wait_ge(w_low, W_STEPS * (s.layer + 1) + 1)
                    qk_tile(QKB[s.p], 1 - par, s.tiles(QKB[s.p]))

                if s.k == 0:
                    pe.wait_ge(w_low, W_STEPS * s.layer + 3)
                pe.wait_ge(yl_kept, s.count(1) + YL_CREDIT)
                pe.wait_ge(z_ready, s.count(0) + Z_CREDIT)
                dense(ps_z[:],
                      lambda r: y_h[:, r * P:(r + 1) * P], lambda r: y_l[:, r * P:(r + 1) * P],
                      lambda r: wp_h[:, r, :], lambda r: wp_l[:, r, :]).then_inc(proj_done, 1)

            run_slots(pe, slot)

        @block.scalar
        def _(act):
            def keep_qk(t, par, layer, count):
                par, t = (par + t // TILES) % 2, t % TILES
                act.wait_ge(qk_done, count)
                dst = k_t[par][:, t, :] if t < KT else q_t[par][:, t - KT, :]
                nc.scalar.activation(dst, ps_qk[t % 2][:], ACT.Identity,
                                     bias=b_qk[:, layer, t:t + 1]).then_inc(qk_kept, 1)

            def keep_xh(par, p):
                nc.scalar.copy(xt_h[par][:, :, p * P:(p + 1) * P],
                               ps_t[:].rearrange("p (t c) -> p t c", t=KT)).then_inc(xh_kept, 1)

            def build_kx(par, p):
                for hh in range(HG):
                    rows = slice(DH * hh, DH * hh + DH)
                    last = nc.scalar.copy(k_x[rows, :, hh, :], k_t[par][rows, :, p * P:(p + 1) * P])
                last.then_inc(kx_built, 1)

            def exp():
                nc.scalar.activation(e_s[:], t_s[:], ACT.Exp, scale=SCALE).then_inc(exp_done, 1)

            def split_w_qk(layer):
                act.wait_ge(w_in, (W_STEPS * layer + 1) * LOADED)
                for t in range(KT):
                    last = nc.scalar.copy(wqk_h[:, t, :], w_stage[:, t, :])
                last.then_inc(w_high, 1)

            def split_w_rest(layer):
                act.wait_ge(w_in, (W_STEPS * layer + 3) * LOADED)
                nc.scalar.copy(wv_h[:], w_stage[:, :, 0:E]).then_inc(w_high, 1)
                if layer:
                    act.wait_ge(proj_done, PAIRS * layer)
                nc.scalar.copy(wp_h[:], w_stage[:, :, E:2 * E]).then_inc(w_high, 1)

            for m in range(AHEAD):
                act.wait_ge(t_done, m + 1)
                keep_xh(m // GROUP, m % GROUP)
            split_w_qk(0)
            act.wait_ge(bias_in, 4 * LAYERS * LOADED)
            for t in range(TILES):
                keep_qk(t, 0, 0, t + 1)
                if t == KT:
                    act.wait_ge(qk_kept, KT)
                    act.wait_ge(zeroed, 1)
                    build_kx(0, 0)
            act.wait_ge(s_done, 1)
            build_kx(0, 1)
            keep_qk(TILES, 0, 0, TILES + 1)
            act.wait_ge(shifted, 1)
            exp()
            split_w_rest(0)

            def slot(s):
                par = (s.k // GROUP) % 2
                a, b = QKA[s.p], QKB[s.p]
                if s.has(s.tile_pair(a)):
                    keep_qk(a, 1 - par, s.pair(s.tile_pair(a))[0], s.tiles(a))
                if s.fixed and s.k == GROUP - 1 and s.layer + 1 < LAYERS:
                    act.wait_ge(qk_done, TILES * PAIRS // GROUP * (s.layer + 1))
                    split_w_qk(s.layer + 1)
                if s.has(AHEAD):
                    act.wait_ge(t_done, s.count(AHEAD + 1))
                    keep_xh(par, s.p)
                act.wait_ge(pv_done, s.count(1))
                nc.scalar.copy(y_h[:], ps_y[:]).then_inc(yh_kept, 1)
                if s.has(2):
                    act.wait_ge(s_done, s.count(2))
                    if s.p == GROUP - 2:
                        act.wait_ge(qk_kept, s.tiles(KT - 1))
                    build_kx(((s.k + 2) // GROUP) % 2, (s.k + 2) % GROUP)
                if s.has(s.tile_pair(b)):
                    keep_qk(b, 1 - par, s.pair(s.tile_pair(b))[0], s.tiles(b))
                if s.has(1):
                    act.wait_ge(shifted, s.count(2))
                    exp()
                b = s.k % 2
                act.wait_ge(rstd_ready, s.count(1))
                act.wait_ge(stored[b], s.ring(-2, 2, 1))
                nc.scalar.activation(z_out[b][:], x_res[b][:], ACT.Identity,
                                     bias=shift[b][:], scale=rstd[b][:]).then_inc(out_ready, 1)

            run_slots(act, slot, between=split_w_rest)

        @block.vector
        def _(dve):
            def across_halves(op, out_tile, first, expect):
                dve.wait_ge(dve_step, expect + first)
                for qd in range(4):
                    o = qd ^ 1
                    last = nc.vector.tensor_copy(red_x[Q * qd:Q * qd + Q, :], red[Q * o:Q * o + Q, :])
                last.then_inc(dve_step, 1)
                dve.wait_ge(dve_step, expect + first + 1)
                nc.vector.tensor_tensor(out_tile[:], red[:], red_x[:], op).then_inc(dve_step, 1)
                dve.wait_ge(dve_step, expect + first + 2)

            SM_STEPS = 8

            def blocks(t):
                return t[:].rearrange("p (c m) -> p c m", m=Q)

            def per_row(t):
                return t[:].unsqueeze(2).to_broadcast([P, H * HALVES, Q])

            def add_mask(steps):
                nc.vector.tensor_tensor(t_s[:].rearrange("p (h c) -> p h c", h=H),
                                        ps_s[:].rearrange("p (h c) -> p h c", h=H),
                                        mask[:].unsqueeze(1).to_broadcast([P, H, NODES]),
                                        ALU.add).then_inc(masked, 1)

            def subtract_max(count, steps):
                dve.wait_ge(masked, count)
                nc.vector.reduce_max(red[:], blocks(t_s), axis=AX.X).then_inc(dve_step, 1)
                across_halves(ALU.max, row_max, 1, steps)
                nc.vector.tensor_tensor(blocks(t_s), blocks(t_s), per_row(row_max),
                                        ALU.subtract).then_inc(shifted, 1)

            def invert_sum(steps):
                nc.vector.reduce_sum(red[:], blocks(e_s), axis=AX.X).then_inc(dve_step, 1)
                across_halves(ALU.add, row_sum, 4, steps)
                nc.vector.reciprocal(row_inv[:], row_sum[:]).then_inc(inv_ready, 1)

            def transpose_p():
                for b in range(2):
                    rows = slice(NODES * b, NODES * b + NODES)
                    last = nc.vector.transpose(p_t[rows, :, b, :],
                                               e_s[rows, :].rearrange("p (h c) -> p h c", h=H))
                last.then_inc(pt_ready, 1)

            def keep_xl(par, p):
                cols = slice(p * P, (p + 1) * P)
                nc.vector.tensor_tensor(xt_l[par][:, :, cols], ps_t[:].rearrange("p (t c) -> p t c", t=KT),
                                        xt_h[par][:, :, cols].bitcast(FP32), ALU.subtract).then_inc(xt_kept, 1)

            def split_w(low, high, stage, count):
                dve.wait_ge(w_high, count)
                nc.vector.tensor_tensor(low, stage, high.bitcast(FP32), ALU.subtract).then_inc(w_low, 1)

            def split_w_rest(layer):
                split_w(wv_l[:], wv_h[:], w_stage[:, :, 0:E], W_STEPS * layer + 2)
                split_w(wp_l[:], wp_h[:], w_stage[:, :, E:2 * E], W_STEPS * layer + 3)

            SOFTMAX = 6
            dve.sem_inc(v_kept, V_CREDIT)
            dve.sem_inc(yl_kept, YL_CREDIT)
            dve.sem_inc(z_ready, Z_CREDIT)
            dve.sem_inc(out_ready, Z_CREDIT)
            nc.vector.memset(k_x[:], 0.0).then_inc(zeroed, 1)
            nc.vector.memset(minus_half[:], -0.5).then_inc(mask_step, 1)
            for b in range(2):
                nc.vector.memset(p_t[NODES * b:NODES * b + NODES, :, 1 - b, :], 0.0).then_inc(mask_step, 1)
            dve.wait_ge(const_in, 6 * LOADED)
            nc.vector.tensor_tensor(mask[:], adj_i[:], eye_s[:], ALU.add).then_inc(mask_step, 1)
            dve.wait_ge(mask_step, 4)
            nc.vector.tensor_scalar(mask[:], mask[:], 0.0, -1.0, ALU.is_gt, ALU.add).then_inc(mask_step, 1)
            dve.wait_ge(mask_step, 5)
            nc.vector.tensor_scalar(mask[:], mask[:], MASKED, None, ALU.mult).then_inc(mask_step, 1)
            for m in range(AHEAD):
                dve.wait_ge(xh_kept, m + 1)
                keep_xl(m // GROUP, m % GROUP)
            split_w(wqk_l[:], wqk_h[:], w_stage[:], 1)
            dve.wait_ge(mask_step, 6)
            dve.wait_ge(s_done, 1)
            add_mask(0)
            subtract_max(1, 0)
            dve.wait_ge(bias_in, 4 * LAYERS * LOADED)
            split_w_rest(0)
            dve.wait_ge(exp_done, 1)
            invert_sum(0)
            dve.wait_ge(normed, 1)
            transpose_p()

            def slot(s):
                par = (s.k // GROUP) % 2
                b = s.k % 2
                dve.wait_ge(v_done, s.count(1))
                nc.vector.tensor_tensor(v_s[b][:], ps_v[:], b_v[:, s.layer, :], ALU.add).then_inc(v_kept, 1)
                if s.has(AHEAD):
                    dve.wait_ge(xh_kept, s.count(AHEAD + 1))
                    keep_xl(par, s.p)
                if s.fixed and s.k == GROUP - 1 and s.layer + 1 < LAYERS:
                    split_w(wqk_l[:], wqk_h[:], w_stage[:], W_STEPS * (s.layer + 1) + 1)
                steps = s.count(1, SOFTMAX)
                if s.has(1):
                    dve.wait_ge(s_done, s.count(2))
                    add_mask(steps)
                dve.wait_ge(yh_kept, s.count(1))
                nc.vector.tensor_tensor(y_l[:], ps_y[:], y_h[:].bitcast(FP32), ALU.subtract).then_inc(yl_kept, 1)
                if s.has(1):
                    subtract_max(s.count(2), steps)
                    dve.wait_ge(exp_done, s.count(2))
                    invert_sum(steps)
                dve.wait_ge(proj_done, s.count(1))
                dve.wait_ge(xb_ready, s.count(1))
                nc.vector.tensor_tensor(x_res[b][:], ps_z[:], x_res[b][:], ALU.add).then_inc(z_ready, 1)
                dve.wait_ge(z_ready, s.count(1) + Z_CREDIT)
                nc.vector.bn_stats(stats[:], x_res[b][:]).then_inc(var_ready, 1)
                dve.wait_ge(var_ready, s.count(0, 2) + 1)
                dve.sem_inc(passed, 1)
                nc.vector.bn_aggr(mean_var[b][:], stats[:]).then_inc(var_ready, 1)
                if s.has(1):
                    dve.wait_ge(normed, s.count(2))
                    dve.wait_ge(pv_done, s.count(1))
                    transpose_p()

            run_slots(dve, slot, between=split_w_rest)

        @block.gpsimd
        def _(pool):
            def normalise():
                e = e_s[:].rearrange("p (c m) -> p c m", m=Q)
                nc.gpsimd.tensor_tensor(e, e, row_inv[:].unsqueeze(2).to_broadcast([P, H * HALVES, Q]),
                                        ALU.mult).then_inc(normed, 1)

            pool.wait_ge(bias_in, 4 * LAYERS * LOADED)
            pool.wait_ge(mask_step, 1)
            pool.wait_ge(inv_ready, 1)
            normalise()

            def slot(s):
                b = s.k % 2
                pool.wait_ge(res_loaded[b], s.ring(0, 2))
                nc.gpsimd.tensor_tensor(x_res[b][:], x_res[b][:], b_p[:, s.layer, :], ALU.add).then_inc(xb_ready, 1)
                if s.has(1):
                    pool.wait_ge(inv_ready, s.count(2))
                    normalise()
                pool.wait_ge(var_ready, s.count(1, 2))
                pool.sem_inc(passed, 1)
                nc.gpsimd.tensor_scalar(var_eps[:], mean_var[b][:, 1:2], EPS, None, ALU.add).then_inc(pool_step, 1)
                pool.wait_ge(pool_step, s.count(0, 2) + 1)
                nc.gpsimd.tensor_tensor(rstd[b][:], var_eps[:], minus_half[:], ALU.pow).then_inc(pool_step, 1)
                pool.wait_ge(pool_step, s.count(0, 2) + 2)
                pool.sem_inc(passed, 1)
                nc.gpsimd.tensor_scalar(shift[b][:], mean_var[b][:, 0:1], rstd[b][:], -1.0,
                                        ALU.mult, ALU.mult).then_inc(rstd_ready, 1)

            run_slots(pool, slot)


def kernel(x, adj, L0_gnn_Wqkv, L0_gnn_bqkv, L0_gnn_Wproj, L0_gnn_bproj,
           L1_gnn_Wqkv, L1_gnn_bqkv, L1_gnn_Wproj, L1_gnn_bproj):
    import concourse.bacc as bacc
    from concourse.bass_utils import run_bass_kernel_spmd

    nc = bacc.Bacc("TRN2", target_bir_lowering=False, num_devices=1)
    arrays = {}

    def give(name, a):
        a = np.ascontiguousarray(a)
        arrays[name] = a
        return nc.dram_tensor(name, a.shape, mybir.dt.from_np(a.dtype), kind="ExternalInput").ap()

    r = np.arange(P)
    c = np.arange(NODES)
    own = (c // Q * Q)[None, :] + (r % Q)[:, None] == ((r // Q % HALVES) * Q)[:, None] + (c % Q)[None, :]
    args = [
        give("x", np.asarray(x).reshape(GRAPHS * NODES, E)),
        give("adj", np.asarray(adj)),
        give("ident", np.eye(P, dtype=np.float32)),
        give("eye", own.astype(np.float32)),
        [[give("wqkv0", L0_gnn_Wqkv), give("bqkv0", L0_gnn_bqkv), give("wproj0", L0_gnn_Wproj), give("bproj0", L0_gnn_bproj)],
         [give("wqkv1", L1_gnn_Wqkv), give("bqkv1", L1_gnn_bqkv), give("wproj1", L1_gnn_Wproj), give("bproj1", L1_gnn_bproj)]],
    ]
    out = nc.dram_tensor("out", [GRAPHS * NODES, E], FP32, kind="ExternalOutput").ap()
    gnn_kernel(nc, *args, out)
    result = run_bass_kernel_spmd(nc, [arrays], core_ids=[0])
    return result.results[0]["out"].reshape(GRAPHS, NODES, E)
```

```python
import numpy as np

import concourse.bass as bass
from concourse import mybir
from contextlib import ExitStack

FP32 = mybir.dt.float32
FP32R = mybir.dt.float32r
INT32 = mybir.dt.int32
ALU = mybir.AluOpType
ACT = mybir.ActivationFunctionType
AX = mybir.AxisListType

GRAPHS, NODES, E, H = 128, 64, 512, 16
DH = E // H
P = 128
LAYERS = 2
Q = 32
PAIRS = GRAPHS * NODES // P
GROUP = 4
TOK = GROUP * P
KT = E // P
HG = P // DH
HALVES = NODES // Q
SLOTS = LAYERS * PAIRS
AHEAD = 2 * GROUP
LOAD = AHEAD + 2
X_RING = 4
UNROLL = 2 * GROUP
LOOPS = PAIRS // UNROLL - 1
TILES = 2 * KT
QKA = [1, 3, 5, 7]
QKB = [2, 4, 6, TILES]
SCALE = float(DH) ** -0.5
EPS = 1e-5
MASKED = 3.0e38
LOADED = 16


def gnn_kernel(nc, x, adj, ident, eye, weights, out):
    ctx = ExitStack()
    with ctx:
        def sb(name, shape, dt=FP32):
            return ctx.enter_context(nc.sbuf_tensor(name, shape, dt))

        def pb(name, shape):
            return ctx.enter_context(nc.psum_tensor(name, shape, FP32))

        def sem(name):
            return ctx.enter_context(nc.semaphore(name))

        hidden = nc.dram_tensor("hidden", [PAIRS * P, E], FP32, kind="Internal").ap()
        sources = [x, hidden]
        targets = [hidden, out]

        w_stage = sb("w_stage", [P, KT, 2 * E])
        wqk_h = sb("wqk_h", [P, KT, 2 * E], FP32R)
        wqk_l = sb("wqk_l", [P, KT, 2 * E], FP32R)
        wv_h = sb("wv_h", [P, KT, E], FP32R)
        wv_l = sb("wv_l", [P, KT, E], FP32R)
        wp_h = sb("wp_h", [P, KT, E], FP32R)
        wp_l = sb("wp_l", [P, KT, E], FP32R)
        b_qk = sb("b_qk", [P, LAYERS, TILES])
        b_v = sb("b_v", [P, LAYERS, E])
        b_p = sb("b_p", [P, LAYERS, E])
        idn = sb("idn", [P, P])
        adj_i = sb("adj_i", [P, NODES], INT32)
        eye_s = sb("eye_s", [P, NODES])
        mask = sb("mask", [P, NODES])
        minus_half = sb("minus_half", [P, 1])

        x_in = [sb(f"x_in{b}", [P, E]) for b in range(4)]
        xt_h = [sb(f"xt_h{b}", [P, KT, TOK], FP32R) for b in range(2)]
        xt_l = [sb(f"xt_l{b}", [P, KT, TOK], FP32R) for b in range(2)]
        q_t = [sb(f"q_t{b}", [P, KT, TOK]) for b in range(2)]
        k_t = [sb(f"k_t{b}", [P, KT, TOK]) for b in range(2)]
        k_x = sb("k_x", [P, KT, HG, P])
        v_s = [sb(f"v_s{b}", [P, E]) for b in range(2)]
        t_s = sb("t_s", [P, H * NODES])
        e_s = sb("e_s", [P, H * NODES])
        p_t = sb("p_t", [P, H, 2, NODES])
        y_h = sb("y_h", [P, E], FP32R)
        y_l = sb("y_l", [P, E], FP32R)
        x_res = [sb(f"x_res{b}", [P, E]) for b in range(2)]
        z_out = [sb(f"z_out{b}", [P, E]) for b in range(2)]
        red = sb("red", [P, H * HALVES])
        red_x = sb("red_x", [P, H * HALVES])
        row_max = sb("row_max", [P, H * HALVES])
        row_sum = sb("row_sum", [P, H * HALVES])
        row_inv = sb("row_inv", [P, H * HALVES])
        stats = sb("stats", [P, 6])
        mean_var = sb("mean_var", [P, 2])
        var_eps = sb("var_eps", [P, 1])
        minus_mean = sb("minus_mean", [P, 1])
        rstd = sb("rstd", [P, 1])

        ps_s = pb("ps_s", [P, H * NODES])
        ps_qk = [pb(f"ps_qk{b}", [P, TOK]) for b in range(2)]
        ps_v = pb("ps_v", [P, E])
        ps_t = pb("ps_t", [P, KT * P])
        ps_y = pb("ps_y", [P, E])
        ps_z = pb("ps_z", [P, E])

        first_banks = [ps_t, ps_y, ps_z, ps_v]

        ident_in = sem("ident_in")
        const_in = sem("const_in")
        bias_in = sem("bias_in")
        wqk_in = [sem(f"wqk_in{t}") for t in range(KT)]
        w_rest_in = sem("w_rest_in")
        x_loaded = [sem(f"x_loaded{b}") for b in range(4)]
        res_loaded = [sem(f"res_loaded{b}") for b in range(2)]
        stored = [sem(f"stored{b}") for b in range(2)]
        zeroed = sem("zeroed")
        mask_step = sem("mask_step")
        wqk_high = sem("wqk_high")
        wqk_low_p = sem("wqk_low_p")
        wqk_low_d = sem("wqk_low_d")
        w_rest_high = sem("w_rest_high")
        w_rest_low = sem("w_rest_low")
        qk_done = sem("qk_done")
        v_done = sem("v_done")
        t_done = sem("t_done")
        s_done = sem("s_done")
        pv_done = sem("pv_done")
        proj_done = sem("proj_done")
        qk_kept = sem("qk_kept")
        xh_kept = sem("xh_kept")
        xt_kept = sem("xt_kept")
        kx_built = sem("kx_built")
        v_kept = sem("v_kept")
        masked = sem("masked")
        dve_step = sem("dve_step")
        shifted = sem("shifted")
        exp_done = sem("exp_done")
        inv_ready = sem("inv_ready")
        normed = sem("normed")
        pt_ready = sem("pt_ready")
        yh_kept = sem("yh_kept")
        yl_kept = sem("yl_kept")
        xb_ready = sem("xb_ready")
        z_ready = sem("z_ready")
        var_ready = sem("var_ready")
        pool_step = sem("pool_step")
        out_ready = sem("out_ready")

        V_CREDIT = YL_CREDIT = Z_CREDIT = 1
        SOFTMAX_STEPS = 6
        POOL_STEPS = 3
        POOL_SPLITS, DVE_SPLITS = (0, 2), (1, 3)

        class Slot:

            def __init__(self, layer, j, k):
                self.layer, self.j, self.k = layer, j, k
                self.p = k % GROUP
                self.last = not isinstance(j, int) or layer * PAIRS + UNROLL * j + k
                self.fixed = isinstance(j, int)

            def count(self, plus=0, each=1):
                return self.j * (UNROLL * each) + each * (self.layer * PAIRS + self.k + plus)

            def ring(self, plus, size, more=0):
                c = (self.layer * PAIRS + self.k + plus) // size + 1 + more
                return self.j * (UNROLL // size * LOADED) + LOADED * c

            def tiles(self, t):
                g = (self.layer * PAIRS + self.k) // GROUP + 1
                return self.j * (UNROLL // GROUP * TILES) + TILES * g + t + 1

            def tile_pair(self, t):
                return GROUP * (1 + t // TILES) - self.p

            def has(self, plus):
                return not self.fixed or self.count(plus) < SLOTS

            def pair(self, plus):
                m = self.layer * PAIRS + self.k + plus
                if self.fixed:
                    m += UNROLL * self.j
                    return m // PAIRS, (m % PAIRS) * P
                return self.layer, self.j * (UNROLL * P) + (self.k + plus) * P

        def run_slots(eng, slot, between=None, loops=LOOPS):
            for layer in range(LAYERS):
                with eng.Fori(0, loops) as j:
                    for k in range(UNROLL):
                        slot(Slot(layer, j, k))
                for j in range(loops, PAIRS // UNROLL):
                    for k in range(UNROLL):
                        slot(Slot(layer, j, k))
                if between is not None and layer + 1 < LAYERS:
                    between(layer + 1)

        def wait_qk_split(eng, layer):
            eng.wait_ge(wqk_low_p, len(POOL_SPLITS) * (layer + 1))
            eng.wait_ge(wqk_low_d, len(DVE_SPLITS) * (layer + 1))

        block = ctx.enter_context(nc.Block())

        passed = sem("passed")
        CONSTS = 5 * LOADED

        @block.sync
        def _(sp):
            def load_x(layer, row, b, count):
                sp.dma_start(x_in[b][:], sources[layer][bass.ds(row, P), :]).then_inc(x_loaded[b], LOADED)

            def load_w_qk(layer):
                w = weights[layer][0].rearrange("(t p) n -> p t n", p=P)
                for t in range(KT):
                    sp.dma_start(w_stage[:, t, :], w[:, t, 0:2 * E]).then_inc(wqk_in[t], LOADED)

            def load_w_rest(layer):
                w = weights[layer][0].rearrange("(t p) n -> p t n", p=P)
                wp = weights[layer][2].rearrange("(t p) n -> p t n", p=P)
                sp.dma_start(w_stage[:, :, 0:E], w[:, :, 2 * E:3 * E]).then_inc(w_rest_in, LOADED)
                sp.dma_start(w_stage[:, :, E:2 * E], wp).then_inc(w_rest_in, LOADED)

            sp.sem_inc(stored[0], LOADED)
            sp.sem_inc(stored[1], LOADED)
            sp.dma_start(idn[:], ident).then_inc(ident_in, LOADED)
            for m in range(4):
                load_x(0, m * P, m, m)
            load_w_qk(0)
            sp.dma_start(eye_s[:], eye).then_inc(const_in, LOADED)
            for b in range(2):
                for mh in range(HALVES):
                    r = Q * (HALVES * b + mh)
                    src = adj.rearrange("(a n) m -> n a m", a=HALVES)[:, :, Q * mh:Q * mh + Q]
                    dst = adj_i[r:r + Q, :].rearrange("p (a m) -> p a m", a=HALVES)
                    sp.dma_start(dst, src).then_inc(const_in, LOADED)
            with nc.allow_non_contiguous_dma(reason="biases by partition, once"):
                for layer in range(LAYERS):
                    b = weights[layer][1]
                    sp.dma_start(b_qk[:, layer, 0:KT], b[E:2 * E].rearrange("(t p) -> p t", p=P)).then_inc(bias_in, LOADED)
                    sp.dma_start(b_qk[:, layer, KT:TILES], b[0:E].rearrange("(t p) -> p t", p=P)).then_inc(bias_in, LOADED)
                    sp.dma_start(b_v[:, layer, :], b[2 * E:3 * E].unsqueeze(0).to_broadcast([P, E])).then_inc(bias_in, LOADED)
                    sp.dma_start(b_p[:, layer, :], weights[layer][3].unsqueeze(0).to_broadcast([P, E])).then_inc(bias_in, LOADED)
            sp.dma_start(x_res[0][:], sources[0][0:P, :]).then_inc(res_loaded[0], LOADED)
            for m in range(4, LOAD):
                sp.wait_ge(t_done, m - 3)
                load_x(0, m * P, m % 4, m)
            wait_qk_split(sp, 0)
            load_w_rest(0)

            def slot(s):
                if s.fixed and s.j == LOOPS and s.layer + 1 < LAYERS and s.k == 0:
                    sp.wait_ge(w_rest_low, 2 * (s.layer + 1))
                    load_w_qk(s.layer + 1)
                if s.has(LOAD):
                    sp.wait_ge(t_done, s.count(LOAD - 3))
                    sp.sem_inc(passed, 1)
                    layer, row = s.pair(LOAD)
                    if layer > 0:
                        sp.wait_ge(stored[s.k % 2], s.ring(LOAD - PAIRS, 2, 1))
                        sp.sem_inc(passed, 1)
                    load_x(layer, row, (s.k + LOAD) % 4, None)
                if s.has(1):
                    sp.wait_ge(out_ready, s.count(0) + Z_CREDIT)
                    sp.sem_inc(passed, 1)
                    layer, row = s.pair(1)
                    if layer > 0:
                        sp.wait_ge(stored[(s.k + 1) % 2], s.ring(1 - PAIRS, 2, 1))
                        sp.sem_inc(passed, 1)
                    sp.dma_start(x_res[(s.k + 1) % 2][:], sources[layer][bass.ds(row, P), :]
                                 ).then_inc(res_loaded[(s.k + 1) % 2], LOADED)
                sp.wait_ge(out_ready, s.count(1) + Z_CREDIT)
                sp.sem_inc(passed, 1)
                layer, row = s.pair(0)
                sp.dma_start(targets[layer][bass.ds(row, P), :], z_out[s.k % 2][:]
                             ).then_inc(stored[s.k % 2], LOADED)
                if s.fixed and s.j == LOOPS and s.layer + 1 < LAYERS and s.k == GROUP:
                    wait_qk_split(sp, s.layer + 1)
                    load_w_rest(s.layer + 1)

            run_slots(sp, slot, loops=LOOPS - 1)
            for b in range(2):
                sp.wait_ge(stored[b], LOADED * (SLOTS // 2 + 1))

        @block.tensor
        def _(pe):
            def dense(ps, lhs_h, lhs_l, rhs_h, rhs_l):
                for t in range(KT):
                    nc.tensor.matmul(ps, lhs_l(t), rhs_h(t), start=(t == 0), stop=False)
                    nc.tensor.matmul(ps, lhs_h(t), rhs_l(t), start=False, stop=False)
                    last = nc.tensor.matmul(ps, lhs_h(t), rhs_h(t), start=False, stop=(t == KT - 1))
                return last

            def transpose_x(b, ps=ps_t):
                for t in range(KT):
                    last = nc.tensor.transpose(ps[:, t * P:(t + 1) * P], x_in[b][:, t * P:(t + 1) * P], idn[:])
                last.then_inc(t_done, 1)

            def qk_tile(t, par, count):
                par, t = (par + t // TILES) % 2, t % TILES
                c0 = E + t * P if t < KT else (t - KT) * P
                if isinstance(count, int) and count <= 2:
                    pass
                else:
                    pe.wait_ge(qk_kept, count - 2)
                dense(ps_qk[t % 2][:],
                      lambda r: wqk_h[:, r, c0:c0 + P], lambda r: wqk_l[:, r, c0:c0 + P],
                      lambda r: xt_h[par][:, r, :], lambda r: xt_l[par][:, r, :]).then_inc(qk_done, 1)

            def scores(par, p):
                for g in range(KT):
                    for nh in range(HALVES):
                        for qd in range(4):
                            b, mh = qd // 2, qd % 2
                            n0 = p * P + b * NODES + nh * Q
                            m0 = b * NODES + mh * Q
                            dst = ps_s[Q * qd:Q * qd + Q, :].rearrange("p (h c) -> p h c", h=H)
                            last = nc.tensor.matmul(
                                dst[:, HG * g:HG * g + HG, nh * Q:nh * Q + Q],
                                q_t[par][:, g, n0:n0 + Q], k_x[:, g, :, m0:m0 + Q],
                                start=True, stop=True)
                last.then_inc(s_done, 1)

            pe.wait_ge(ident_in, LOADED)
            for m in range(AHEAD):
                pe.wait_ge(x_loaded[m % 4], LOADED * (m // 4 + 1))
                if m >= len(first_banks):
                    pe.wait_ge(xt_kept, m + 1 - len(first_banks))
                transpose_x(m % 4, first_banks[m % len(first_banks)])
            wait_qk_split(pe, 0)
            for t in range(TILES):
                qk_tile(t, 0, t + 1)
            pe.wait_ge(qk_kept, TILES)
            pe.wait_ge(kx_built, 1)
            scores(0, 0)
            qk_tile(TILES, 0, TILES + 1)

            def slot(s):
                par = (s.k // GROUP) % 2
                if s.has(s.tile_pair(QKA[s.p])):
                    qk_tile(QKA[s.p], 1 - par, s.tiles(QKA[s.p]))

                if s.k == 0:
                    pe.wait_ge(w_rest_low, 2 * s.layer + 1)
                pe.wait_ge(v_kept, s.count(0) + V_CREDIT)
                tok = slice(s.p * P, s.p * P + P)
                dense(ps_v[:],
                      lambda r: xt_h[par][:, r, tok], lambda r: xt_l[par][:, r, tok],
                      lambda r: wv_h[:, r, :], lambda r: wv_l[:, r, :]).then_inc(v_done, 1)

                if s.has(AHEAD):
                    pe.wait_ge(x_loaded[s.k % 4], s.ring(AHEAD, 4))
                    pe.wait_ge(xt_kept, s.count(AHEAD))
                    transpose_x(s.k % 4)

                if s.has(1):
                    if s.p == GROUP - 1:
                        pe.wait_ge(qk_kept, s.tiles(TILES - 1))
                    pe.wait_ge(kx_built, s.count(2))
                    pe.wait_ge(masked, s.count(1))
                    scores(((s.k + 1) // GROUP) % 2, (s.k + 1) % GROUP)

                pe.wait_ge(v_kept, s.count(1) + V_CREDIT)
                pe.wait_ge(pt_ready, s.count(1))
                pe.wait_ge(yl_kept, s.count(0) + YL_CREDIT)
                for g in range(KT):
                    for hh in range(HG):
                        h = HG * g + hh
                        last = nc.tensor.matmul(ps_y[DH * hh:DH * hh + DH, g * P:(g + 1) * P],
                                                v_s[s.k % 2][:, DH * h:DH * h + DH],
                                                p_t[:, h, :, :].rearrange("p b n -> p (b n)"),
                                                start=True, stop=True)
                last.then_inc(pv_done, 1)

                if s.has(s.tile_pair(QKB[s.p])):
                    if s.p == GROUP - 1:
                        pe.wait_ge(xt_kept, s.count(AHEAD + 1))
                        if s.fixed and s.k == GROUP - 1 and s.layer + 1 < LAYERS:
                            wait_qk_split(pe, s.layer + 1)
                    qk_tile(QKB[s.p], 1 - par, s.tiles(QKB[s.p]))

                if s.k == 0:
                    pe.wait_ge(w_rest_low, 2 * s.layer + 2)
                pe.wait_ge(yl_kept, s.count(1) + YL_CREDIT)
                pe.wait_ge(z_ready, s.count(0) + Z_CREDIT)
                dense(ps_z[:],
                      lambda r: y_h[:, r * P:(r + 1) * P], lambda r: y_l[:, r * P:(r + 1) * P],
                      lambda r: wp_h[:, r, :], lambda r: wp_l[:, r, :]).then_inc(proj_done, 1)

            run_slots(pe, slot)

        @block.scalar
        def _(act):
            def keep_qk(t, par, layer, count):
                par, t = (par + t // TILES) % 2, t % TILES
                act.wait_ge(qk_done, count)
                dst = k_t[par][:, t, :] if t < KT else q_t[par][:, t - KT, :]
                nc.scalar.activation(dst, ps_qk[t % 2][:], ACT.Identity,
                                     bias=b_qk[:, layer, t:t + 1]).then_inc(qk_kept, 1)

            def keep_xh(par, p, ps=ps_t):
                nc.scalar.copy(xt_h[par][:, :, p * P:(p + 1) * P],
                               ps[:].rearrange("p (t c) -> p t c", t=KT)).then_inc(xh_kept, 1)

            def build_kx(par, p):
                for hh in range(HG):
                    rows = slice(DH * hh, DH * hh + DH)
                    last = nc.scalar.copy(k_x[rows, :, hh, :], k_t[par][rows, :, p * P:(p + 1) * P])
                last.then_inc(kx_built, 1)

            def exp():
                nc.scalar.activation(e_s[:], t_s[:], ACT.Exp, scale=SCALE).then_inc(exp_done, 1)

            def split_w_qk(layer):
                for t in range(KT):
                    act.wait_ge(wqk_in[t], LOADED * (layer + 1))
                    nc.scalar.copy(wqk_h[:, t, :], w_stage[:, t, :]).then_inc(wqk_high, 1)

            def split_w_v(layer):
                act.wait_ge(w_rest_in, 2 * LOADED * (layer + 1))
                nc.scalar.copy(wv_h[:], w_stage[:, :, 0:E]).then_inc(w_rest_high, 1)

            def split_w_proj(layer):
                if layer:
                    act.wait_ge(proj_done, PAIRS * layer)
                nc.scalar.copy(wp_h[:], w_stage[:, :, E:2 * E]).then_inc(w_rest_high, 1)

            for m in range(AHEAD):
                act.wait_ge(t_done, m + 1)
                keep_xh(m // GROUP, m % GROUP, first_banks[m % len(first_banks)])
            split_w_qk(0)
            act.wait_ge(bias_in, 4 * LAYERS * LOADED)
            for t in range(TILES):
                keep_qk(t, 0, 0, t + 1)
                if t == KT:
                    act.wait_ge(qk_kept, KT)
                    act.wait_ge(zeroed, 1)
                    build_kx(0, 0)
            split_w_v(0)
            act.wait_ge(s_done, 1)
            build_kx(0, 1)
            keep_qk(TILES, 0, 0, TILES + 1)
            act.wait_ge(shifted, 1)
            exp()
            split_w_proj(0)

            def slot(s):
                par = (s.k // GROUP) % 2
                a, b = QKA[s.p], QKB[s.p]
                if s.has(s.tile_pair(a)):
                    keep_qk(a, 1 - par, s.pair(s.tile_pair(a))[0], s.tiles(a))
                if s.fixed and s.k == GROUP - 1 and s.layer + 1 < LAYERS:
                    act.wait_ge(qk_done, TILES * PAIRS // GROUP * (s.layer + 1))
                    split_w_qk(s.layer + 1)
                if s.has(AHEAD):
                    act.wait_ge(t_done, s.count(AHEAD + 1))
                    keep_xh(par, s.p)
                if s.fixed and s.j == LOOPS and s.k == UNROLL - 1 and s.layer + 1 < LAYERS:
                    act.wait_ge(v_done, PAIRS * (s.layer + 1))
                    split_w_v(s.layer + 1)
                act.wait_ge(pv_done, s.count(1))
                nc.scalar.copy(y_h[:], ps_y[:]).then_inc(yh_kept, 1)
                if s.has(2):
                    act.wait_ge(s_done, s.count(2))
                    if s.p == GROUP - 2:
                        act.wait_ge(qk_kept, s.tiles(KT - 1))
                    build_kx(((s.k + 2) // GROUP) % 2, (s.k + 2) % GROUP)
                if s.has(s.tile_pair(b)):
                    keep_qk(b, 1 - par, s.pair(s.tile_pair(b))[0], s.tiles(b))
                if s.has(1):
                    act.wait_ge(shifted, s.count(2))
                    exp()

            run_slots(act, slot, between=split_w_proj)

        @block.vector
        def _(dve):
            def across_halves(op, out_tile, first, expect):
                dve.wait_ge(dve_step, expect + first)
                for qd in range(4):
                    o = qd ^ 1
                    last = nc.vector.tensor_copy(red_x[Q * qd:Q * qd + Q, :], red[Q * o:Q * o + Q, :])
                last.then_inc(dve_step, 1)
                dve.wait_ge(dve_step, expect + first + 1)
                nc.vector.tensor_tensor(out_tile[:], red[:], red_x[:], op).then_inc(dve_step, 1)
                dve.wait_ge(dve_step, expect + first + 2)

            def blocks(t):
                return t[:].rearrange("p (c m) -> p c m", m=Q)

            def per_row(t):
                return t[:].unsqueeze(2).to_broadcast([P, H * HALVES, Q])

            def add_mask(steps):
                nc.vector.tensor_tensor(t_s[:].rearrange("p (h c) -> p h c", h=H),
                                        ps_s[:].rearrange("p (h c) -> p h c", h=H),
                                        mask[:].unsqueeze(1).to_broadcast([P, H, NODES]),
                                        ALU.add).then_inc(masked, 1)

            def subtract_max(count, steps):
                dve.wait_ge(masked, count)
                nc.vector.reduce_max(red[:], blocks(t_s), axis=AX.X).then_inc(dve_step, 1)
                across_halves(ALU.max, row_max, 1, steps)
                nc.vector.tensor_tensor(blocks(t_s), blocks(t_s), per_row(row_max),
                                        ALU.subtract).then_inc(shifted, 1)

            def invert_sum(steps):
                nc.vector.reduce_sum(red[:], blocks(e_s), axis=AX.X).then_inc(dve_step, 1)
                across_halves(ALU.add, row_sum, 4, steps)
                nc.vector.reciprocal(row_inv[:], row_sum[:]).then_inc(inv_ready, 1)

            def transpose_p():
                for b in range(2):
                    rows = slice(NODES * b, NODES * b + NODES)
                    last = nc.vector.transpose(p_t[rows, :, b, :],
                                               e_s[rows, :].rearrange("p (h c) -> p h c", h=H))
                last.then_inc(pt_ready, 1)

            def keep_xl(par, p, ps=ps_t):
                cols = slice(p * P, (p + 1) * P)
                nc.vector.tensor_tensor(xt_l[par][:, :, cols], ps[:].rearrange("p (t c) -> p t c", t=KT),
                                        xt_h[par][:, :, cols].bitcast(FP32), ALU.subtract).then_inc(xt_kept, 1)

            def split_qk_low(layer):
                for t in DVE_SPLITS:
                    dve.wait_ge(wqk_high, KT * layer + t + 1)
                    nc.vector.tensor_tensor(wqk_l[:, t, :], w_stage[:, t, :], wqk_h[:, t, :].bitcast(FP32),
                                            ALU.subtract).then_inc(wqk_low_d, 1)

            dve.sem_inc(v_kept, V_CREDIT)
            dve.sem_inc(yl_kept, YL_CREDIT)
            dve.sem_inc(z_ready, Z_CREDIT)
            nc.vector.memset(k_x[:], 0.0).then_inc(zeroed, 1)
            nc.vector.memset(minus_half[:], -0.5).then_inc(mask_step, 1)
            for b in range(2):
                nc.vector.memset(p_t[NODES * b:NODES * b + NODES, :, 1 - b, :], 0.0).then_inc(mask_step, 1)
            dve.wait_ge(const_in, CONSTS)
            nc.vector.tensor_tensor(mask[:], adj_i[:], eye_s[:], ALU.add).then_inc(mask_step, 1)
            dve.wait_ge(mask_step, 4)
            nc.vector.tensor_scalar(mask[:], mask[:], 0.0, -1.0, ALU.is_gt, ALU.add).then_inc(mask_step, 1)
            dve.wait_ge(mask_step, 5)
            nc.vector.tensor_scalar(mask[:], mask[:], MASKED, None, ALU.mult).then_inc(mask_step, 1)
            for m in range(AHEAD):
                dve.wait_ge(xh_kept, m + 1)
                keep_xl(m // GROUP, m % GROUP, first_banks[m % len(first_banks)])
            split_qk_low(0)
            dve.wait_ge(mask_step, 6)
            dve.wait_ge(s_done, 1)
            add_mask(0)
            subtract_max(1, 0)
            dve.wait_ge(bias_in, 4 * LAYERS * LOADED)
            dve.wait_ge(exp_done, 1)
            invert_sum(0)
            dve.wait_ge(normed, 1)
            transpose_p()

            def slot(s):
                par = (s.k // GROUP) % 2
                b = s.k % 2
                dve.wait_ge(v_done, s.count(1))
                nc.vector.tensor_tensor(v_s[b][:], ps_v[:], b_v[:, s.layer, :], ALU.add).then_inc(v_kept, 1)
                if s.has(AHEAD):
                    dve.wait_ge(xh_kept, s.count(AHEAD + 1))
                    keep_xl(par, s.p)
                if s.fixed and s.k == GROUP - 1 and s.layer + 1 < LAYERS:
                    split_qk_low(s.layer + 1)
                steps = s.count(1, SOFTMAX_STEPS)
                if s.has(1):
                    dve.wait_ge(s_done, s.count(2))
                    add_mask(steps)
                dve.wait_ge(yh_kept, s.count(1))
                nc.vector.tensor_tensor(y_l[:], ps_y[:], y_h[:].bitcast(FP32), ALU.subtract).then_inc(yl_kept, 1)
                if s.has(1):
                    subtract_max(s.count(2), steps)
                    dve.wait_ge(exp_done, s.count(2))
                    invert_sum(steps)
                dve.wait_ge(proj_done, s.count(1))
                dve.wait_ge(xb_ready, s.count(1))
                nc.vector.tensor_tensor(x_res[b][:], ps_z[:], x_res[b][:], ALU.add).then_inc(z_ready, 1)
                dve.wait_ge(z_ready, s.count(1) + Z_CREDIT)
                nc.vector.bn_stats(stats[:], x_res[b][:]).then_inc(var_ready, 1)
                dve.wait_ge(var_ready, s.count(0, 2) + 1)
                dve.sem_inc(passed, 1)
                nc.vector.bn_aggr(mean_var[:], stats[:]).then_inc(var_ready, 1)
                if s.has(1):
                    dve.wait_ge(normed, s.count(2))
                    dve.wait_ge(pv_done, s.count(1))
                    transpose_p()

            run_slots(dve, slot)

        @block.gpsimd
        def _(pool):
            def normalise():
                e = e_s[:].rearrange("p (c m) -> p c m", m=Q)
                nc.gpsimd.tensor_tensor(e, e, row_inv[:].unsqueeze(2).to_broadcast([P, H * HALVES, Q]),
                                        ALU.mult).then_inc(normed, 1)

            def low_part(low, stage, high):
                return nc.gpsimd.tensor_tensor(low, stage, high.bitcast(FP32), ALU.subtract)

            def split_qk_low(layer):
                for t in POOL_SPLITS:
                    pool.wait_ge(wqk_high, KT * layer + t + 1)
                    low_part(wqk_l[:, t, :], w_stage[:, t, :], wqk_h[:, t, :]).then_inc(wqk_low_p, 1)

            def split_rest_low(layer):
                pool.wait_ge(w_rest_high, 2 * layer + 1)
                low_part(wv_l[:], w_stage[:, :, 0:E], wv_h[:]).then_inc(w_rest_low, 1)
                pool.wait_ge(w_rest_high, 2 * layer + 2)
                low_part(wp_l[:], w_stage[:, :, E:2 * E], wp_h[:]).then_inc(w_rest_low, 1)

            pool.sem_inc(out_ready, Z_CREDIT)
            split_qk_low(0)
            pool.wait_ge(bias_in, 4 * LAYERS * LOADED)
            pool.wait_ge(mask_step, 1)
            split_rest_low(0)
            pool.wait_ge(inv_ready, 1)
            normalise()

            def slot(s):
                b = s.k % 2
                pool.wait_ge(res_loaded[b], s.ring(0, 2))
                nc.gpsimd.tensor_tensor(x_res[b][:], x_res[b][:], b_p[:, s.layer, :], ALU.add).then_inc(xb_ready, 1)
                if s.fixed and s.k == GROUP - 1 and s.layer + 1 < LAYERS:
                    split_qk_low(s.layer + 1)
                if s.has(1):
                    pool.wait_ge(inv_ready, s.count(2))
                    normalise()
                pool.wait_ge(var_ready, s.count(1, 2))
                pool.sem_inc(passed, 1)
                nc.gpsimd.tensor_scalar(var_eps[:], mean_var[:, 1:2], EPS, None, ALU.add).then_inc(pool_step, 1)
                nc.gpsimd.tensor_scalar(minus_mean[:], mean_var[:, 0:1], -1.0, None, ALU.mult).then_inc(pool_step, 1)
                pool.wait_ge(pool_step, s.count(0, POOL_STEPS) + 2)
                nc.gpsimd.tensor_tensor(rstd[:], var_eps[:], minus_half[:], ALU.pow).then_inc(pool_step, 1)
                pool.wait_ge(pool_step, s.count(0, POOL_STEPS) + 3)
                pool.wait_ge(stored[b], s.ring(-2, 2, 1))
                pool.sem_inc(passed, 1)
                nc.gpsimd.tensor_scalar(z_out[b][:], x_res[b][:], minus_mean[:], rstd[:],
                                        ALU.add, ALU.mult).then_inc(out_ready, 1)
                if s.fixed and s.k == UNROLL - 1 and s.layer + 1 < LAYERS:
                    split_rest_low(s.layer + 1)

            run_slots(pool, slot)


def kernel(x, adj, L0_gnn_Wqkv, L0_gnn_bqkv, L0_gnn_Wproj, L0_gnn_bproj,
           L1_gnn_Wqkv, L1_gnn_bqkv, L1_gnn_Wproj, L1_gnn_bproj):
    import concourse.bacc as bacc
    from concourse.bass_utils import run_bass_kernel_spmd

    nc = bacc.Bacc("TRN2", target_bir_lowering=False, num_devices=1)
    arrays = {}

    def give(name, a):
        a = np.ascontiguousarray(a)
        arrays[name] = a
        return nc.dram_tensor(name, a.shape, mybir.dt.from_np(a.dtype), kind="ExternalInput").ap()

    r = np.arange(P)
    c = np.arange(NODES)
    own = (c // Q * Q)[None, :] + (r % Q)[:, None] == ((r // Q % HALVES) * Q)[:, None] + (c % Q)[None, :]
    args = [
        give("x", np.asarray(x).reshape(GRAPHS * NODES, E)),
        give("adj", np.asarray(adj)),
        give("ident", np.eye(P, dtype=np.float32)),
        give("eye", own.astype(np.float32)),
        [[give("wqkv0", L0_gnn_Wqkv), give("bqkv0", L0_gnn_bqkv), give("wproj0", L0_gnn_Wproj), give("bproj0", L0_gnn_bproj)],
         [give("wqkv1", L1_gnn_Wqkv), give("bqkv1", L1_gnn_bqkv), give("wproj1", L1_gnn_Wproj), give("bproj1", L1_gnn_bproj)]],
    ]
    out = nc.dram_tensor("out", [GRAPHS * NODES, E], FP32, kind="ExternalOutput").ap()
    gnn_kernel(nc, *args, out)
    result = run_bass_kernel_spmd(nc, [arrays], core_ids=[0])
    return result.results[0]["out"].reshape(GRAPHS, NODES, E)
```

```python
import numpy as np

import concourse.bass as bass
from concourse import mybir
from contextlib import ExitStack

FP32 = mybir.dt.float32
FP32R = mybir.dt.float32r
INT32 = mybir.dt.int32
ALU = mybir.AluOpType
ACT = mybir.ActivationFunctionType
AX = mybir.AxisListType

GRAPHS, NODES, E, H = 128, 64, 512, 16
DH = E // H
P = 128
LAYERS = 2
Q = 32
PAIRS = GRAPHS * NODES // P
GROUP = 4
TOK = GROUP * P
KT = E // P
HG = P // DH
HALVES = NODES // Q
SLOTS = LAYERS * PAIRS
AHEAD = 2 * GROUP
LOAD = AHEAD + 2
UNROLL = 2 * GROUP
LOOPS = PAIRS // UNROLL - 1
TILES = 2 * KT
QKA = [[2], [4], [6], []]
QKM = [[], [], [7], []]
QKB = [[3], [5], [], [TILES, TILES + 1]]
SCALE = float(DH) ** -0.5
EPS = 1e-5
MASKED = 3.0e38
LOADED = 16


def gnn_kernel(nc, x, x_t, adj, ident, eye, weights, out):
    ctx = ExitStack()
    with ctx:
        def sb(name, shape, dt=FP32):
            return ctx.enter_context(nc.sbuf_tensor(name, shape, dt))

        def pb(name, shape):
            return ctx.enter_context(nc.psum_tensor(name, shape, FP32))

        def sem(name):
            return ctx.enter_context(nc.semaphore(name))

        hidden = nc.dram_tensor("hidden", [PAIRS * P, E], FP32, kind="Internal").ap()
        sources = [x, hidden]
        t_sources = [x_t, hidden]
        targets = [hidden, out]

        w_stage = sb("w_stage", [P, KT, 2 * E])
        wqk_h = sb("wqk_h", [P, KT, 2 * E], FP32R)
        wqk_l = sb("wqk_l", [P, KT, 2 * E], FP32R)
        wv_h = sb("wv_h", [P, KT, E], FP32R)
        wv_l = sb("wv_l", [P, KT, E], FP32R)
        wp_h = sb("wp_h", [P, KT, E], FP32R)
        wp_l = sb("wp_l", [P, KT, E], FP32R)
        b_qk = sb("b_qk", [P, LAYERS, TILES])
        b_v = sb("b_v", [P, LAYERS, E])
        b_p = sb("b_p", [P, LAYERS, E])
        idn = sb("idn", [P, P])
        adj_i = sb("adj_i", [P, NODES], INT32)
        eye_s = sb("eye_s", [P, NODES])
        mask = sb("mask", [P, NODES])
        minus_half = sb("minus_half", [P, 1])

        x_in = [sb(f"x_in{b}", [P, E]) for b in range(4)]
        xt_h = [sb(f"xt_h{b}", [P, KT, TOK], FP32R) for b in range(2)]
        xt_l = [sb(f"xt_l{b}", [P, KT, TOK], FP32R) for b in range(2)]
        q_t = [sb(f"q_t{b}", [P, KT, TOK]) for b in range(2)]
        k_t = [sb(f"k_t{b}", [P, KT, TOK]) for b in range(2)]
        k_x = sb("k_x", [P, KT, HG, P])
        v_s = [sb(f"v_s{b}", [P, E]) for b in range(2)]
        t_s = sb("t_s", [P, H * NODES])
        e_s = [sb(f"e_s{b}", [P, H * NODES]) for b in range(2)]
        p_t = sb("p_t", [P, H, 2, NODES])
        y_h = sb("y_h", [P, E], FP32R)
        y_l = sb("y_l", [P, E], FP32R)
        x_res = [sb(f"x_res{b}", [P, E]) for b in range(2)]
        z_out = [sb(f"z_out{b}", [P, E]) for b in range(2)]
        red = sb("red", [P, H * HALVES])
        red_x = sb("red_x", [P, H * HALVES])
        row_max = sb("row_max", [P, H])
        row_sum = sb("row_sum", [P, H * HALVES])
        row_inv = sb("row_inv", [P, H * HALVES])
        stats = sb("stats", [P, 6])
        mean_var = sb("mean_var", [P, 2])
        var_eps = sb("var_eps", [P, 1])
        minus_mean = sb("minus_mean", [P, 1])
        rstd = sb("rstd", [P, 1])

        ps_s = pb("ps_s", [P, H * NODES])
        ps_qk = [pb(f"ps_qk{b}", [P, TOK]) for b in range(2)]
        ps_v = pb("ps_v", [P, E])
        ps_t = pb("ps_t", [P, KT * P])
        ps_y = pb("ps_y", [P, E])
        ps_z = pb("ps_z", [P, E])

        ident_in = sem("ident_in")
        const_in = sem("const_in")
        bias_in = sem("bias_in")
        bias_qk_in = sem("bias_qk_in")
        wk_in = [sem(f"wk_in{half}") for half in range(2)]
        wq_in = sem("wq_in")
        w_rest_in = sem("w_rest_in")
        x_loaded = [sem(f"x_loaded{b}") for b in range(4)]
        res_loaded = [sem(f"res_loaded{b}") for b in range(2)]
        stored = [sem(f"stored{b}") for b in range(2)]
        zeroed = sem("zeroed")
        mask_step = sem("mask_step")
        w_high = sem("w_high")
        wk_low = sem("wk_low")
        wq_low = sem("wq_low")
        wv_low = sem("wv_low")
        wp_low = sem("wp_low")
        qk_done = sem("qk_done")
        v_done = sem("v_done")
        t_done = sem("t_done")
        s_done = sem("s_done")
        pv_done = sem("pv_done")
        proj_done = sem("proj_done")
        qk_kept = sem("qk_kept")
        xh_kept = sem("xh_kept")
        xt_kept = sem("xt_kept")
        kx_built = sem("kx_built")
        v_kept = sem("v_kept")
        masked = sem("masked")
        dve_step = sem("dve_step")
        shifted = sem("shifted")
        exp_done = sem("exp_done")
        inv_ready = sem("inv_ready")
        normed = sem("normed")
        pt_ready = sem("pt_ready")
        yh_kept = sem("yh_kept")
        yl_kept = sem("yl_kept")
        xb_ready = sem("xb_ready")
        z_ready = sem("z_ready")
        var_ready = sem("var_ready")
        pool_step = sem("pool_step")
        out_ready = sem("out_ready")

        V_CREDIT = YL_CREDIT = Z_CREDIT = 1
        SOFTMAX_STEPS = 4
        POOL_STEPS = 3
        W_HIGHS = 5
        Q_COLS = slice(0, E)
        K_HALVES = [slice(E, E + E // 2), slice(E + E // 2, 2 * E)]

        class Slot:

            def __init__(self, layer, j, k):
                self.layer, self.j, self.k = layer, j, k
                self.p = k % GROUP
                self.last = not isinstance(j, int) or layer * PAIRS + UNROLL * j + k
                self.fixed = isinstance(j, int)

            def count(self, plus=0, each=1):
                return self.j * (UNROLL * each) + each * (self.layer * PAIRS + self.k + plus)

            def ring(self, plus, size, more=0):
                c = (self.layer * PAIRS + self.k + plus) // size + 1 + more
                return self.j * (UNROLL // size * LOADED) + LOADED * c

            def tiles(self, t):
                g = (self.layer * PAIRS + self.k) // GROUP + 1
                return self.j * (UNROLL // GROUP * TILES) + TILES * g + t + 1

            def tile_pair(self, t):
                return GROUP * (1 + t // TILES) - self.p

            def has(self, plus):
                return not self.fixed or self.count(plus) < SLOTS

            def pair(self, plus):
                m = self.layer * PAIRS + self.k + plus
                if self.fixed:
                    m += UNROLL * self.j
                    return m // PAIRS, (m % PAIRS) * P
                return self.layer, self.j * (UNROLL * P) + (self.k + plus) * P

        def run_slots(eng, slot, between=None, loops=LOOPS):
            for layer in range(LAYERS):
                with eng.Fori(0, loops) as j:
                    for k in range(UNROLL):
                        slot(Slot(layer, j, k))
                for j in range(loops, PAIRS // UNROLL):
                    for k in range(UNROLL):
                        slot(Slot(layer, j, k))
                if between is not None and layer + 1 < LAYERS:
                    between(layer + 1)

        def v_ahead(s, plus):
            return not s.has(GROUP + plus)

        def wait_qk_split(eng, layer):
            eng.wait_ge(wk_low, 2 * (layer + 1))
            eng.wait_ge(wq_low, layer + 1)

        block = ctx.enter_context(nc.Block())

        passed = sem("passed")
        CONSTS = 3 * LOADED

        @block.sync
        def _(sp):
            def load_x(layer, row, b):
                sp.dma_start(x_in[b][:], t_sources[layer][bass.ds(row, P), :]).then_inc(x_loaded[b], LOADED)

            def load_w_k(layer, half):
                w = weights[layer][0].rearrange("(t p) n -> p t n", p=P)
                cols = K_HALVES[half]
                sp.dma_start(w_stage[:, :, cols], w[:, :, cols]).then_inc(wk_in[half], LOADED)

            def load_w_q(layer):
                w = weights[layer][0].rearrange("(t p) n -> p t n", p=P)
                sp.dma_start(w_stage[:, :, Q_COLS], w[:, :, 0:E]).then_inc(wq_in, LOADED)

            def load_w_rest(layer):
                w = weights[layer][0].rearrange("(t p) n -> p t n", p=P)
                wp = weights[layer][2].rearrange("(t p) n -> p t n", p=P)
                sp.dma_start(w_stage[:, :, 0:E], w[:, :, 2 * E:3 * E]).then_inc(w_rest_in, LOADED)
                sp.dma_start(w_stage[:, :, E:2 * E], wp).then_inc(w_rest_in, LOADED)

            sp.sem_inc(stored[0], LOADED)
            sp.sem_inc(stored[1], LOADED)
            load_w_k(0, 0)
            for m in range(4):
                load_x(0, m * P, m)
            load_w_k(0, 1)
            load_w_q(0)
            with nc.allow_non_contiguous_dma(reason="biases by partition, once"):
                for layer in range(LAYERS):
                    b = weights[layer][1][0:2 * E].rearrange("(t p) -> p t", p=P)
                    sp.dma_start(b_qk[:, layer, :], b).then_inc(bias_qk_in, LOADED)
            for m in range(4, 8):
                sp.wait_ge(xt_kept, m - 3)
                load_x(0, m * P, m % 4)
            sp.dma_start(eye_s[:], eye).then_inc(const_in, LOADED)
            for b in range(2):
                sp.dma_start(adj_i[b * NODES:(b + 1) * NODES, :], adj).then_inc(const_in, LOADED)
            for layer in range(LAYERS):
                b = weights[layer][1][2 * E:3 * E]
                sp.dma_start(b_v[:, layer, :], b.unsqueeze(0).to_broadcast([P, E])).then_inc(bias_in, LOADED)
                sp.dma_start(b_p[:, layer, :], weights[layer][3].unsqueeze(0).to_broadcast([P, E])).then_inc(bias_in, LOADED)
            sp.dma_start(x_res[0][:], sources[0][0:P, :]).then_inc(res_loaded[0], LOADED)
            sp.dma_start(idn[:], ident).then_inc(ident_in, LOADED)
            wait_qk_split(sp, 0)
            load_w_rest(0)
            for m in range(8, LOAD):
                sp.wait_ge(xt_kept, m - 3)
                load_x(0, m * P, m % 4)

            def slot(s):
                if s.fixed and s.j == LOOPS and s.layer + 1 < LAYERS and s.k == 0:
                    sp.wait_ge(wv_low, s.layer + 1)
                    sp.wait_ge(wp_low, s.layer + 1)
                    for half in range(2):
                        load_w_k(s.layer + 1, half)
                    load_w_q(s.layer + 1)
                if s.has(LOAD):
                    sp.wait_ge(xt_kept, s.count(LOAD - 3))
                    sp.sem_inc(passed, 1)
                    layer, row = s.pair(LOAD)
                    if layer > 0:
                        sp.wait_ge(stored[s.k % 2], s.ring(LOAD - PAIRS, 2, 1))
                        sp.sem_inc(passed, 1)
                    load_x(layer, row, (s.k + LOAD) % 4)
                if s.has(1):
                    sp.wait_ge(out_ready, s.count(0) + Z_CREDIT)
                    sp.sem_inc(passed, 1)
                    layer, row = s.pair(1)
                    if layer > 0:
                        sp.wait_ge(stored[(s.k + 1) % 2], s.ring(1 - PAIRS, 2, 1))
                        sp.sem_inc(passed, 1)
                    sp.dma_start(x_res[(s.k + 1) % 2][:], sources[layer][bass.ds(row, P), :]
                                 ).then_inc(res_loaded[(s.k + 1) % 2], LOADED)
                sp.wait_ge(out_ready, s.count(1) + Z_CREDIT)
                sp.sem_inc(passed, 1)
                layer, row = s.pair(0)
                sp.dma_start(targets[layer][bass.ds(row, P), :], z_out[s.k % 2][:]
                             ).then_inc(stored[s.k % 2], LOADED)
                if s.fixed and s.j == LOOPS and s.layer + 1 < LAYERS and s.k == GROUP:
                    wait_qk_split(sp, s.layer + 1)
                    load_w_rest(s.layer + 1)

            run_slots(sp, slot, loops=LOOPS - 1)
            for b in range(2):
                sp.wait_ge(stored[b], LOADED * (SLOTS // 2 + 1))

        @block.tensor
        def _(pe):
            def dense(ps, lhs_h, lhs_l, rhs_h, rhs_l):
                for t in range(KT):
                    nc.tensor.matmul(ps, lhs_l(t), rhs_h(t), start=(t == 0), stop=False)
                    nc.tensor.matmul(ps, lhs_h(t), rhs_l(t), start=False, stop=False)
                    last = nc.tensor.matmul(ps, lhs_h(t), rhs_h(t), start=False, stop=(t == KT - 1))
                return last

            def transpose_x(b):
                for t in range(KT):
                    last = nc.tensor.transpose(ps_t[:, t * P:(t + 1) * P], x_in[b][:, t * P:(t + 1) * P], idn[:])
                last.then_inc(t_done, 1)

            def qk_tile(t, par, count):
                par, t = (par + t // TILES) % 2, t % TILES
                c0 = E + t * P if t < KT else (t - KT) * P
                if isinstance(count, int) and count <= 2:
                    pass
                else:
                    pe.wait_ge(qk_kept, count - 2)
                dense(ps_qk[t % 2][:],
                      lambda r: wqk_h[:, r, c0:c0 + P], lambda r: wqk_l[:, r, c0:c0 + P],
                      lambda r: xt_h[par][:, r, :], lambda r: xt_l[par][:, r, :]).then_inc(qk_done, 1)

            def scores(par, p):
                for g in range(KT):
                    for b in range(2):
                        for nh in range(HALVES):
                            r, n0 = Q * (HALVES * b + nh), p * P + b * NODES + nh * Q
                            last = nc.tensor.matmul(
                                ps_s[r:r + Q, g * HG * NODES:(g + 1) * HG * NODES].rearrange("p (h m) -> p h m", h=HG),
                                q_t[par][:, g, n0:n0 + Q], k_x[:, g, :, b * NODES:(b + 1) * NODES],
                                start=True, stop=True)
                last.then_inc(s_done, 1)

            pe.wait_ge(xt_kept, GROUP)
            for t in range(TILES):
                if t == 0:
                    pe.wait_ge(wk_low, 1)
                if t == KT // 2:
                    pe.wait_ge(wk_low, 2)
                if t == KT:
                    pe.wait_ge(wq_low, 1)
                qk_tile(t, 0, t + 1)
            pe.wait_ge(qk_kept, TILES)
            pe.wait_ge(kx_built, 1)
            scores(0, 0)
            pe.wait_ge(xt_kept, AHEAD)
            qk_tile(TILES, 0, TILES + 1)
            pe.wait_ge(kx_built, 2)
            pe.wait_ge(masked, 1)
            scores(0, 1)
            qk_tile(TILES + 1, 0, TILES + 2)

            def next_tiles(s, tiles):
                for t in tiles:
                    if s.has(s.tile_pair(t)):
                        if t == TILES:
                            pe.wait_ge(xt_kept, s.count(AHEAD + 1))
                            if s.fixed and s.k < GROUP and s.layer + 1 < LAYERS:
                                pe.wait_ge(wk_low, 2 * s.layer + 3)
                        if t == KT // 2 and s.fixed and s.k == GROUP and s.layer + 1 < LAYERS:
                            pe.wait_ge(wk_low, 2 * s.layer + 4)
                        if t == KT and s.fixed and s.k > GROUP and s.layer + 1 < LAYERS:
                            pe.wait_ge(wq_low, s.layer + 2)
                        qk_tile(t, 1 - (s.k // GROUP) % 2, s.tiles(t))

            def next_scores(s):
                if s.has(2):
                    if s.p == GROUP - 2:
                        pe.wait_ge(qk_kept, s.tiles(TILES - 1))
                    pe.wait_ge(kx_built, s.count(3))
                    pe.wait_ge(masked, s.count(2))
                    scores(((s.k + 2) // GROUP) % 2, (s.k + 2) % GROUP)

            def values(s, plus):
                par, p = ((s.k + plus) // GROUP) % 2, (s.k + plus) % GROUP
                tok = slice(p * P, p * P + P)
                pe.wait_ge(v_kept, s.count(plus) + V_CREDIT)
                dense(ps_v[:],
                      lambda r: xt_h[par][:, r, tok], lambda r: xt_l[par][:, r, tok],
                      lambda r: wv_h[:, r, :], lambda r: wv_l[:, r, :]).then_inc(v_done, 1)

            def slot(s):
                next_tiles(s, QKA[s.p])

                if s.k == 0:
                    pe.wait_ge(wv_low, s.layer + 1)
                if not v_ahead(s, 0):
                    values(s, 0)
                next_tiles(s, QKM[s.p])

                if s.has(AHEAD) and s.pair(AHEAD)[0] > 0:
                    pe.wait_ge(ident_in, LOADED)
                    pe.wait_ge(x_loaded[s.k % 4], s.ring(AHEAD, 4))
                    pe.wait_ge(xt_kept, s.count(AHEAD))
                    transpose_x(s.k % 4)

                late = bool(QKM[s.p])
                if not late:
                    next_scores(s)
                pe.wait_ge(v_kept, s.count(1) + V_CREDIT)
                pe.wait_ge(pt_ready, s.count(1))
                pe.wait_ge(yl_kept, s.count(0) + YL_CREDIT)
                for g in range(KT):
                    for hh in range(HG):
                        h = HG * g + hh
                        last = nc.tensor.matmul(ps_y[DH * hh:DH * hh + DH, g * P:(g + 1) * P],
                                                v_s[s.k % 2][:, DH * h:DH * h + DH],
                                                p_t[:, h, :, :].rearrange("p b n -> p (b n)"),
                                                start=True, stop=True)
                last.then_inc(pv_done, 1)
                if late:
                    next_scores(s)
                next_tiles(s, QKB[s.p])
                if s.has(1) and v_ahead(s, 1):
                    values(s, 1)

                if s.k == 0:
                    pe.wait_ge(wp_low, s.layer + 1)
                pe.wait_ge(yl_kept, s.count(1) + YL_CREDIT)
                pe.wait_ge(z_ready, s.count(0) + Z_CREDIT)
                dense(ps_z[:],
                      lambda r: y_h[:, r * P:(r + 1) * P], lambda r: y_l[:, r * P:(r + 1) * P],
                      lambda r: wp_h[:, r, :], lambda r: wp_l[:, r, :]).then_inc(proj_done, 1)

            run_slots(pe, slot)

        @block.scalar
        def _(act):
            def keep_qk(t, par, layer, count):
                par, t = (par + t // TILES) % 2, t % TILES
                act.wait_ge(qk_done, count)
                c = (t + KT) % TILES
                dst = k_t[par][:, t, :] if t < KT else q_t[par][:, t - KT, :]
                nc.scalar.activation(dst, ps_qk[t % 2][:], ACT.Identity,
                                     bias=b_qk[:, layer, c:c + 1]).then_inc(qk_kept, 1)

            def keep_xh(par, p, src):
                nc.scalar.copy(xt_h[par][:, :, p * P:(p + 1) * P],
                               src[:].rearrange("p (t c) -> p t c", t=KT)).then_inc(xh_kept, 1)

            def build_kx(par, p):
                for hh in range(HG):
                    rows = slice(DH * hh, DH * hh + DH)
                    last = nc.scalar.copy(k_x[rows, :, hh, :], k_t[par][rows, :, p * P:(p + 1) * P])
                last.then_inc(kx_built, 1)

            def exp(b, halves=(0, 1)):
                t = t_s[:].rearrange("p (h c m) -> p h c m", h=H, c=HALVES)
                e = e_s[b][:].rearrange("p (h c m) -> p h c m", h=H, c=HALVES)
                for g in halves:
                    for nh in range(HALVES):
                        for mh in range(HALVES):
                            r_n, r_m = Q * (HALVES * g + nh), Q * (HALVES * g + mh)
                            last = nc.scalar.activation(e[r_m:r_m + Q, :, nh, :], t[r_n:r_n + Q, :, mh, :],
                                                        ACT.Exp, scale=SCALE)
                if g:
                    last.then_inc(exp_done, 1)

            def split_w_k(layer, half):
                cols = K_HALVES[half]
                act.wait_ge(wk_in[half], LOADED * (layer + 1))
                nc.scalar.copy(wqk_h[:, :, cols], w_stage[:, :, cols]).then_inc(w_high, 1)

            def split_w_q(layer):
                act.wait_ge(wq_in, LOADED * (layer + 1))
                nc.scalar.copy(wqk_h[:, :, Q_COLS], w_stage[:, :, Q_COLS]).then_inc(w_high, 1)

            def split_w_v(layer):
                act.wait_ge(w_rest_in, 2 * LOADED * (layer + 1))
                nc.scalar.copy(wv_h[:], w_stage[:, :, 0:E]).then_inc(w_high, 1)

            def split_w_proj(layer):
                if layer:
                    act.wait_ge(proj_done, PAIRS * layer)
                nc.scalar.copy(wp_h[:], w_stage[:, :, E:2 * E]).then_inc(w_high, 1)

            split_w_k(0, 0)
            for m in range(GROUP):
                act.wait_ge(x_loaded[m], LOADED)
                keep_xh(0, m, x_in[m])
            split_w_k(0, 1)
            split_w_q(0)
            for m in range(GROUP, AHEAD):
                act.wait_ge(x_loaded[m % 4], 2 * LOADED)
                keep_xh(1, m - GROUP, x_in[m % 4])
            act.wait_ge(bias_qk_in, LAYERS * LOADED)
            for t in range(TILES):
                keep_qk(t, 0, 0, t + 1)
                if t == KT:
                    act.wait_ge(qk_kept, KT)
                    act.wait_ge(zeroed, 1)
                    build_kx(0, 0)
                if t == TILES - 2:
                    split_w_v(0)
            split_w_proj(0)
            act.wait_ge(s_done, 1)
            build_kx(0, 1)
            keep_qk(TILES, 0, 0, TILES + 1)
            act.wait_ge(shifted, 1)
            exp(0)
            act.wait_ge(s_done, 2)
            build_kx(0, 2)
            keep_qk(TILES + 1, 0, 0, TILES + 2)
            act.wait_ge(shifted, 2)
            exp(1)

            def keep_next_xh(s, plus):
                k = s.k + plus
                if s.pair(AHEAD + plus)[0] > 0:
                    act.wait_ge(t_done, s.count(AHEAD + plus + 1 - PAIRS))
                    keep_xh((k // GROUP) % 2, k % GROUP, ps_t)
                else:
                    act.wait_ge(v_done, s.count(plus + 1))
                    act.wait_ge(x_loaded[k % 4], s.ring(AHEAD + plus, 4))
                    keep_xh((k // GROUP) % 2, k % GROUP, x_in[k % 4])

            def keep_tiles(s, tiles):
                for t in tiles:
                    if s.has(s.tile_pair(t)):
                        keep_qk(t, 1 - (s.k // GROUP) % 2, s.pair(s.tile_pair(t))[0], s.tiles(t))

            def slot(s):
                switch = s.fixed and s.j == LOOPS and s.layer + 1 < LAYERS
                keep_tiles(s, QKA[s.p])
                keep_tiles(s, QKM[s.p])
                if switch and s.k == GROUP - 2:
                    act.wait_ge(qk_done, TILES * PAIRS // GROUP * (s.layer + 1))
                    for half in range(2):
                        split_w_k(s.layer + 1, half)
                if s.has(AHEAD) and s.p != GROUP - 1:
                    keep_next_xh(s, 0)
                if switch and s.k == UNROLL - 1:
                    act.wait_ge(v_done, PAIRS * (s.layer + 1))
                    split_w_v(s.layer + 1)
                act.wait_ge(pv_done, s.count(1))
                nc.scalar.copy(y_h[:], ps_y[:]).then_inc(yh_kept, 1)
                if s.has(3):
                    act.wait_ge(s_done, s.count(3))
                    if s.p == GROUP - 3:
                        act.wait_ge(qk_kept, s.tiles(KT - 1))
                    build_kx(((s.k + 3) // GROUP) % 2, (s.k + 3) % GROUP)
                if switch and s.k == GROUP - 1:
                    split_w_q(s.layer + 1)
                keep_tiles(s, QKB[s.p])
                if s.has(2):
                    act.wait_ge(shifted, s.count(3))
                    exp(s.k % 2, (0,))
                    if s.p == GROUP - 2 and s.has(AHEAD + 1):
                        keep_next_xh(s, 1)
                    exp(s.k % 2, (1,))

            run_slots(act, slot, between=split_w_proj)

        @block.vector
        def _(dve):
            def across_halves(steps):
                dve.wait_ge(dve_step, steps + 1)
                for qd in range(4):
                    o = qd ^ 1
                    last = nc.vector.tensor_copy(red_x[Q * qd:Q * qd + Q, :], red[Q * o:Q * o + Q, :])
                last.then_inc(dve_step, 1)
                dve.wait_ge(dve_step, steps + 2)
                nc.vector.tensor_tensor(row_sum[:], red[:], red_x[:], ALU.add).then_inc(dve_step, 1)
                dve.wait_ge(dve_step, steps + 3)

            def add_mask():
                nc.vector.tensor_tensor(t_s[:].rearrange("p (h c) -> p h c", h=H),
                                        ps_s[:].rearrange("p (h c) -> p h c", h=H),
                                        mask[:].unsqueeze(1).to_broadcast([P, H, NODES]),
                                        ALU.add).then_inc(masked, 1)

            def subtract_max(count, steps):
                t = t_s[:].rearrange("p (h c) -> p h c", h=H)
                dve.wait_ge(masked, count)
                nc.vector.reduce_max(row_max[:], t, axis=AX.X).then_inc(dve_step, 1)
                dve.wait_ge(dve_step, steps + 1)
                nc.vector.tensor_tensor(t, t, row_max[:].unsqueeze(2).to_broadcast([P, H, NODES]),
                                        ALU.subtract).then_inc(shifted, 1)

            def invert_sum(b, steps):
                nc.vector.reduce_sum(red[:], e_s[b][:].rearrange("p (c m) -> p c m", m=Q), axis=AX.X).then_inc(dve_step, 1)
                across_halves(steps)
                nc.vector.reciprocal(row_inv[:], row_sum[:]).then_inc(inv_ready, 1)

            def transpose_p(b):
                for g in range(2):
                    rows = slice(NODES * g, NODES * g + NODES)
                    last = nc.vector.transpose(p_t[rows, :, g, :],
                                               e_s[b][rows, :].rearrange("p (h c) -> p h c", h=H))
                last.then_inc(pt_ready, 1)

            def keep_xl(par, p, src):
                cols = slice(p * P, (p + 1) * P)
                nc.vector.tensor_tensor(xt_l[par][:, :, cols], src[:].rearrange("p (t c) -> p t c", t=KT),
                                        xt_h[par][:, :, cols].bitcast(FP32), ALU.subtract).then_inc(xt_kept, 1)

            def low_part(low, stage, high):
                return nc.vector.tensor_tensor(low, stage, high.bitcast(FP32), ALU.subtract)

            dve.sem_inc(v_kept, V_CREDIT)
            dve.sem_inc(yl_kept, YL_CREDIT)
            dve.sem_inc(z_ready, Z_CREDIT)
            nc.vector.memset(k_x[:], 0.0).then_inc(zeroed, 1)
            nc.vector.memset(minus_half[:], -0.5).then_inc(mask_step, 1)
            for b in range(2):
                nc.vector.memset(p_t[NODES * b:NODES * b + NODES, :, 1 - b, :], 0.0).then_inc(mask_step, 1)
            for m in range(AHEAD):
                if m in (0, GROUP):
                    half = m // GROUP
                    cols = K_HALVES[half]
                    dve.wait_ge(w_high, half + 1)
                    low_part(wqk_l[:, :, cols], w_stage[:, :, cols], wqk_h[:, :, cols]).then_inc(wk_low, 1)
                dve.wait_ge(xh_kept, m + 1)
                keep_xl(m // GROUP, m % GROUP, x_in[m % 4])
            dve.wait_ge(const_in, CONSTS)
            nc.vector.tensor_tensor(mask[:], adj_i[:], eye_s[:], ALU.add).then_inc(mask_step, 1)
            dve.wait_ge(mask_step, 4)
            nc.vector.tensor_scalar(mask[:], mask[:], 0.0, -1.0, ALU.is_gt, ALU.add).then_inc(mask_step, 1)
            dve.wait_ge(mask_step, 5)
            nc.vector.tensor_scalar(mask[:], mask[:], MASKED, None, ALU.mult).then_inc(mask_step, 1)
            dve.wait_ge(mask_step, 6)
            dve.wait_ge(s_done, 1)
            add_mask()
            subtract_max(1, 0)
            dve.wait_ge(w_high, W_HIGHS)
            low_part(wp_l[:], w_stage[:, :, E:2 * E], wp_h[:]).then_inc(wp_low, 1)
            dve.wait_ge(bias_in, 2 * LAYERS * LOADED)
            dve.wait_ge(exp_done, 1)
            invert_sum(0, 1)
            dve.wait_ge(s_done, 2)
            add_mask()
            subtract_max(2, SOFTMAX_STEPS)
            dve.wait_ge(normed, 1)
            transpose_p(0)

            def keep_next_xl(s, plus):
                k = s.k + plus
                dve.wait_ge(xh_kept, s.count(AHEAD + plus + 1))
                keep_xl((k // GROUP) % 2, k % GROUP, ps_t if s.pair(AHEAD + plus)[0] > 0 else x_in[k % 4])

            def v_early(s, plus):
                return (s.k + plus) % GROUP == GROUP - 1 or v_ahead(s, plus)

            def keep_v(s, plus):
                dve.wait_ge(v_done, s.count(plus + 1))
                nc.vector.tensor_tensor(v_s[(s.k + plus) % 2][:], ps_v[:], b_v[:, s.layer, :], ALU.add).then_inc(v_kept, 1)

            def slot(s):
                b = s.k % 2
                steps = s.count(1, SOFTMAX_STEPS) + 1
                if not v_early(s, 0):
                    keep_v(s, 0)
                if s.has(1) and QKM[s.p]:
                    dve.wait_ge(exp_done, s.count(2))
                    invert_sum(1 - b, steps)
                if s.has(AHEAD) and s.p != GROUP - 1:
                    keep_next_xl(s, 0)
                if s.has(1) and not QKM[s.p]:
                    dve.wait_ge(exp_done, s.count(2))
                    invert_sum(1 - b, steps)
                dve.wait_ge(yh_kept, s.count(1))
                nc.vector.tensor_tensor(y_l[:], ps_y[:], y_h[:].bitcast(FP32), ALU.subtract).then_inc(yl_kept, 1)
                if s.has(2):
                    dve.wait_ge(s_done, s.count(3))
                    add_mask()
                    subtract_max(s.count(3), steps + 3)
                if s.has(1) and v_ahead(s, 1):
                    keep_v(s, 1)
                if s.has(1):
                    dve.wait_ge(normed, s.count(2))
                    dve.wait_ge(pv_done, s.count(1))
                    transpose_p(1 - b)
                if s.has(1) and v_early(s, 1) and not v_ahead(s, 1):
                    keep_v(s, 1)
                if s.p == GROUP - 2 and s.has(AHEAD + 1):
                    keep_next_xl(s, 1)
                dve.wait_ge(proj_done, s.count(1))
                dve.wait_ge(xb_ready, s.count(1))
                nc.vector.tensor_tensor(x_res[b][:], ps_z[:], x_res[b][:], ALU.add).then_inc(z_ready, 1)
                dve.wait_ge(z_ready, s.count(1) + Z_CREDIT)
                nc.vector.bn_stats(stats[:], x_res[b][:]).then_inc(var_ready, 1)
                dve.wait_ge(var_ready, s.count(0, 2) + 1)
                dve.sem_inc(passed, 1)
                nc.vector.bn_aggr(mean_var[:], stats[:]).then_inc(var_ready, 1)

            run_slots(dve, slot)

        @block.gpsimd
        def _(pool):
            def normalise(b):
                e = e_s[b][:].rearrange("p (c m) -> p c m", m=Q)
                nc.gpsimd.tensor_tensor(e, e, row_inv[:].unsqueeze(2).to_broadcast([P, H * HALVES, Q]),
                                        ALU.mult).then_inc(normed, 1)

            def low_part(low, stage, high):
                return nc.gpsimd.tensor_tensor(low, stage, high.bitcast(FP32), ALU.subtract)

            def split_k_low(layer):
                for i, cols in enumerate(K_HALVES):
                    pool.wait_ge(w_high, W_HIGHS * layer + i + 1)
                    low_part(wqk_l[:, :, cols], w_stage[:, :, cols], wqk_h[:, :, cols]).then_inc(wk_low, 1)

            def split_q_low(layer):
                pool.wait_ge(w_high, W_HIGHS * layer + 3)
                low_part(wqk_l[:, :, Q_COLS], w_stage[:, :, Q_COLS], wqk_h[:, :, Q_COLS]).then_inc(wq_low, 1)

            def split_v_low(layer):
                pool.wait_ge(w_high, W_HIGHS * layer + 4)
                low_part(wv_l[:], w_stage[:, :, 0:E], wv_h[:]).then_inc(wv_low, 1)

            pool.sem_inc(out_ready, Z_CREDIT)
            split_q_low(0)
            pool.wait_ge(bias_in, 2 * LAYERS * LOADED)
            pool.wait_ge(mask_step, 1)
            split_v_low(0)
            pool.wait_ge(inv_ready, 1)
            normalise(0)

            def slot(s):
                b = s.k % 2
                pool.wait_ge(res_loaded[b], s.ring(0, 2))
                nc.gpsimd.tensor_tensor(x_res[b][:], x_res[b][:], b_p[:, s.layer, :], ALU.add).then_inc(xb_ready, 1)
                if s.fixed and s.k == GROUP - 1 and s.layer + 1 < LAYERS:
                    split_q_low(s.layer + 1)
                if s.fixed and s.k == UNROLL - 1 and s.layer + 1 < LAYERS:
                    split_v_low(s.layer + 1)
                if s.has(1):
                    pool.wait_ge(inv_ready, s.count(2))
                    normalise(1 - b)
                if s.fixed and s.k == GROUP - 2 and s.layer + 1 < LAYERS:
                    split_k_low(s.layer + 1)
                pool.wait_ge(var_ready, s.count(1, 2))
                pool.sem_inc(passed, 1)
                nc.gpsimd.tensor_scalar(var_eps[:], mean_var[:, 1:2], EPS, None, ALU.add).then_inc(pool_step, 1)
                nc.gpsimd.tensor_scalar(minus_mean[:], mean_var[:, 0:1], -1.0, None, ALU.mult).then_inc(pool_step, 1)
                pool.wait_ge(pool_step, s.count(0, POOL_STEPS) + 2)
                nc.gpsimd.tensor_tensor(rstd[:], var_eps[:], minus_half[:], ALU.pow).then_inc(pool_step, 1)
                pool.wait_ge(pool_step, s.count(0, POOL_STEPS) + 3)
                pool.wait_ge(stored[b], s.ring(-2, 2, 1))
                pool.sem_inc(passed, 1)
                nc.gpsimd.tensor_scalar(z_out[b][:], x_res[b][:], minus_mean[:], rstd[:],
                                        ALU.add, ALU.mult).then_inc(out_ready, 1)
                if s.fixed and s.k == UNROLL - 1 and s.layer + 1 < LAYERS:
                    pool.wait_ge(w_high, W_HIGHS * (s.layer + 2))
                    low_part(wp_l[:], w_stage[:, :, E:2 * E], wp_h[:]).then_inc(wp_low, 1)

            run_slots(pool, slot)


def kernel(x, adj, L0_gnn_Wqkv, L0_gnn_bqkv, L0_gnn_Wproj, L0_gnn_bproj,
           L1_gnn_Wqkv, L1_gnn_bqkv, L1_gnn_Wproj, L1_gnn_bproj):
    import concourse.bacc as bacc
    from concourse.bass_utils import run_bass_kernel_spmd

    nc = bacc.Bacc("TRN2", target_bir_lowering=False, num_devices=1)
    arrays = {}

    def give(name, a):
        a = np.ascontiguousarray(a)
        arrays[name] = a
        return nc.dram_tensor(name, a.shape, mybir.dt.from_np(a.dtype), kind="ExternalInput").ap()

    args = [
        give("x", np.asarray(x).reshape(GRAPHS * NODES, E)),
        give("x_t", np.asarray(x).reshape(PAIRS, P, KT, P).transpose(0, 3, 2, 1).reshape(PAIRS * P, E)),
        give("adj", np.asarray(adj)),
        give("ident", np.eye(P, dtype=np.float32)),
        give("eye", np.tile(np.eye(NODES, dtype=np.float32), (P // NODES, 1))),
        [[give("wqkv0", L0_gnn_Wqkv), give("bqkv0", L0_gnn_bqkv), give("wproj0", L0_gnn_Wproj), give("bproj0", L0_gnn_bproj)],
         [give("wqkv1", L1_gnn_Wqkv), give("bqkv1", L1_gnn_bqkv), give("wproj1", L1_gnn_Wproj), give("bproj1", L1_gnn_bproj)]],
    ]
    out = nc.dram_tensor("out", [GRAPHS * NODES, E], FP32, kind="ExternalOutput").ap()
    gnn_kernel(nc, *args, out)
    result = run_bass_kernel_spmd(nc, [arrays], core_ids=[0])
    return result.results[0]["out"].reshape(GRAPHS, NODES, E)
```
